# Optimizing a Trainium2 kernel written in Bass

```python
import numpy as np
import jax
import jax.numpy as jnp

def _softmax(x, axis=-1):
    return jax.nn.softmax(x, axis=axis)

def _gelu(x):
    return jax.nn.gelu(x, approximate=True)

def _silu(x):
    return jax.nn.silu(x)

def _sigmoid(x):
    return jax.nn.sigmoid(x)

def _layernorm(x, axis=-1, eps=1e-05):
    m = jnp.mean(x, axis=axis, keepdims=True)
    v = jnp.var(x, axis=axis, keepdims=True)
    return (x - m) / jnp.sqrt(v + eps)

def _scatter_add(tgt, idx, src, axis=0):
    return tgt.at[idx].add(src)

def _segment_sum(src, seg, n):
    return jax.ops.segment_sum(src, seg, n)
kernel_name = 'mk_seq_postln_d1_jaxref_r4_ce3286'

def setup_inputs(seed: int=0):
    np.random.seed(seed)
    _w = jnp.asarray

    def _L0_attn_setup():
        import jax, jax.numpy as jnp
        import numpy as np
        NUM_HEADS = 16
        ENCODER_DIM = 256
        HEAD_DIM = ENCODER_DIM // NUM_HEADS
        BATCH, SEQ_LEN = (2, 512)

        def alibi_slopes(num_heads):
            x = (2.0 ** 8) ** (1.0 / num_heads)
            return jnp.asarray([1.0 / x ** (i + 1) for i in range(num_heads)], dtype=jnp.float32)
        key = jax.random.key(seed)
        ks = jax.random.split(key, 9)
        d = ENCODER_DIM
        s = 0.02
        return {'inputs': jax.random.normal(ks[0], (BATCH, SEQ_LEN, d), dtype=jnp.float32), 'Wq': jax.random.normal(ks[1], (d, d), dtype=jnp.float32) * s, 'bq': jax.random.normal(ks[2], (d,), dtype=jnp.float32) * s, 'Wk': jax.random.normal(ks[3], (d, d), dtype=jnp.float32) * s, 'bk': jax.random.normal(ks[4], (d,), dtype=jnp.float32) * s, 'Wv': jax.random.normal(ks[5], (d, d), dtype=jnp.float32) * s, 'bv': jax.random.normal(ks[6], (d,), dtype=jnp.float32) * s, 'Wo': jax.random.normal(ks[7], (d, d), dtype=jnp.float32) * s, 'bo': jax.random.normal(ks[8], (d,), dtype=jnp.float32) * s}
    _L0_attn_in = _L0_attn_setup()

    def _L0_ffn_setup():
        import jax, jax.numpy as jnp
        import numpy as np
        E = 8
        key = jax.random.key(seed)
        k0, k1, k2, k3 = jax.random.split(key, 4)
        B, S, H, F = (4, 1024, 256, 1024)
        x = jax.random.normal(k0, (B, S, H), jnp.float32)
        Wr = jax.random.normal(k1, (E, H), jnp.float32) * 0.02
        W1 = jax.random.normal(k2, (E, H, F), jnp.float32) * 0.02
        b1 = jnp.zeros((E, F), jnp.float32)
        W2 = jax.random.normal(k3, (E, F, H), jnp.float32) * 0.02
        b2 = jnp.zeros((E, H), jnp.float32)
        return {'x': x, 'Wr': Wr, 'W1': W1, 'b1': b1, 'W2': W2, 'b2': b2}
    _L0_ffn_in = _L0_ffn_setup()
    _d = {'L0_attn_inputs': _L0_attn_in['inputs'], 'L0_attn_Wq': _L0_attn_in['Wq'], 'L0_attn_bq': _L0_attn_in['bq'], 'L0_attn_Wk': _L0_attn_in['Wk'], 'L0_attn_bk': _L0_attn_in['bk'], 'L0_attn_Wv': _L0_attn_in['Wv'], 'L0_attn_bv': _L0_attn_in['bv'], 'L0_attn_Wo': _L0_attn_in['Wo'], 'L0_attn_bo': _L0_attn_in['bo'], 'L0_ffn_Wr': _L0_ffn_in['Wr'], 'L0_ffn_W1': _L0_ffn_in['W1'], 'L0_ffn_b1': _L0_ffn_in['b1'], 'L0_ffn_W2': _L0_ffn_in['W2'], 'L0_ffn_b2': _L0_ffn_in['b2']}
    _x0 = _d['L0_attn_inputs']
    _d['L0_attn_inputs'] = jax.random.normal(jax.random.fold_in(jax.random.key(seed), 1), (16, 512, 256), dtype=_x0.dtype)
    del _x0
    return _d

def reference(L0_attn_inputs, L0_attn_Wq, L0_attn_bq, L0_attn_Wk, L0_attn_bk, L0_attn_Wv, L0_attn_bv, L0_attn_Wo, L0_attn_bo, L0_ffn_Wr, L0_ffn_W1, L0_ffn_b1, L0_ffn_W2, L0_ffn_b2):

    def _L0_attn_ref(inputs, Wq, bq, Wk, bk, Wv, bv, Wo, bo):
        import jax, jax.numpy as jnp
        import numpy as np
        NUM_HEADS = 16
        ENCODER_DIM = 256
        HEAD_DIM = ENCODER_DIM // NUM_HEADS
        BATCH, SEQ_LEN = (2, 512)

        def alibi_slopes(num_heads):
            x = (2.0 ** 8) ** (1.0 / num_heads)
            return jnp.asarray([1.0 / x ** (i + 1) for i in range(num_heads)], dtype=jnp.float32)
        B, S, E = inputs.shape
        H, D = (NUM_HEADS, E // NUM_HEADS)

        def split_heads(x):
            return x.reshape(B, S, H, D).transpose(0, 2, 1, 3)
        q = split_heads(inputs @ Wq + bq)
        k = split_heads(inputs @ Wk + bk)
        v = split_heads(inputs @ Wv + bv)
        pos = jnp.arange(S)
        rel = (pos[None, :] - pos[None, :].T).astype(jnp.float32)
        bias = alibi_slopes(H)[:, None, None] * rel
        scale = 1.0 / jnp.sqrt(jnp.asarray(D, dtype=q.dtype))
        scores = jnp.einsum('bhqd,bhkd->bhqk', q, k) * scale + bias[None]
        attn = jax.nn.softmax(scores, axis=-1)
        ctx = jnp.einsum('bhqk,bhkd->bhqd', attn, v)
        ctx = ctx.transpose(0, 2, 1, 3).reshape(B, S, E)
        return ctx @ Wo + bo

    def _L0_ffn_ref(x, Wr, W1, b1, W2, b2):
        import jax, jax.numpy as jnp
        import numpy as np
        E = 8
        B, S, H = x.shape
        xf = x.reshape(-1, H)
        probs = jax.nn.softmax(xf @ Wr.T, axis=-1)
        eid = E - 1
        h = jax.nn.gelu(xf @ W1[eid] + b1[eid], approximate=False)
        y = (h @ W2[eid] + b2[eid]) * probs[:, eid:eid + 1]
        return y.reshape(B, S, H)
    x = L0_attn_inputs
    x = _layernorm(x + _L0_attn_ref(x, L0_attn_Wq, L0_attn_bq, L0_attn_Wk, L0_attn_bk, L0_attn_Wv, L0_attn_bv, L0_attn_Wo, L0_attn_bo), axis=-1)
    x = _layernorm(x + _L0_ffn_ref(x, L0_ffn_Wr, L0_ffn_W1, L0_ffn_b1, L0_ffn_W2, L0_ffn_b2), axis=-1)
    return x

_drawn_inputs = setup_inputs


def setup_inputs(seed=0):
    import zlib

    import numpy as np

    out = dict(_drawn_inputs(seed))
    spreads = {'L0_ffn_b1': (0.0, 0.8), 'L0_ffn_b2': (0.0, 0.601)}
    factors = {'L0_attn_Wq': 8.0,
     'L0_attn_bq': 35.298,
     'L0_attn_Wk': 8.0,
     'L0_attn_bk': 64.0,
     'L0_attn_bv': 8.0,
     'L0_attn_bo': 2.939,
     'L0_ffn_Wr': 8.0,
     'L0_ffn_W1': 3.968,
     'L0_ffn_W2': 3.695}
    for name, (base, spread) in spreads.items():
        noise = np.random.default_rng([zlib.crc32(name.encode()), seed]).standard_normal(out[name].shape)
        drawn = base * np.exp(spread * noise) if base else spread * noise
        out[name] = jnp.asarray(drawn.astype(out[name].dtype))
    for name, factor in factors.items():
        out[name] = (out[name] * factor).astype(out[name].dtype)
    return out
```

```python
from contextlib import ExitStack

import concourse.bass as bass
from concourse import mybir

F32 = mybir.dt.float32
F32R = mybir.dt.float32r
BF16 = mybir.dt.bfloat16
ALU = mybir.AluOpType
ACT = mybir.ActivationFunctionType
AX_X = mybir.AxisListType.X

P = 128
BATCH, SEQ, DIM = 16, 512, 256
HEADS, HEAD_DIM = 16, 16
TILES = SEQ // P
CH = DIM // P
GROUPS = HEADS // 4
EXPERTS, HIDDEN = 8, 1024
HC = HIDDEN // P
EPS = 1e-5
QSCALE = HEAD_DIM ** -0.5

Q_PARTS = (0, 0, 1, 1, 0, 2)
K_PARTS = (0, 1, 0, 1, 2, 0)
ROW_BIAS = len(Q_PARTS) * HEAD_DIM
ROW_MAX = ROW_BIAS + 3
ROWS_MAX = ROW_MAX
ROWS_EXP = ROW_MAX + 2

STEPS = 64

BEFORE, BEHIND = -1, STEPS
SIDE = {BEFORE: [("xt", 0), ("xt", 1), ("pv", 0), ("proj", 0), ("proj", 1), ("proj", 2), ("proj", 3)],
        1: [("v", 0)], 3: [("v", 1)],
        5: [("ct", 0)], 8: [("ct", 1)], 11: [("ct", 2)], 14: [("ct", 3)], 20: [("cb", 0)], 24: [("cb", 1)],
        28: [("wo", 0)], 32: [("wo", 1)], 34: [("ln", 0)], 42: [("norm", 0)], BEHIND: [("nm", 0)]}
INPUT_SIDE = ("xt", "proj", "v", "nm")
MAX_FROM, MAX_TO = 7, 63


def maxima_of(u):
    if not MAX_FROM <= u < MAX_TO:
        return range(0)
    n, span = HEADS * TILES // 2, MAX_TO - MAX_FROM
    return range(n * (u - MAX_FROM) // span, n * (u - MAX_FROM + 1) // span)


class Linear:

    def __init__(self, pair, step, start):
        self.pair, self.step, self.start = pair, step, start

    def __add__(self, n):
        return Linear(self.pair, self.step, self.start + n)

    def __sub__(self, n):
        return self + -n

    def __mul__(self, n):
        return Linear(self.pair, self.step * n, self.start * n)


def count(x):
    return x.pair * x.step + x.start if isinstance(x, Linear) else x


def wait(eng, semaphore, x):
    if isinstance(x, Linear) or x > 0:
        eng.wait_ge(semaphore, count(x))


def attention(nc, io, y1, q_parts_dram, k_parts_dram, m_parts_dram):
    with ExitStack() as ctx:
        def sb(name, shape, dt=F32):
            return ctx.enter_context(nc.sbuf_tensor(name, shape, dt))

        def ps(name, shape):
            return ctx.enter_context(nc.psum_tensor(name, shape, F32))

        def sem(name):
            return ctx.enter_context(nc.semaphore(name))

        ident = sb("ident", [P, P])
        w_raw = sb("w_raw", [P, CH, DIM])
        w_hi = sb("w_hi", [P, 4, CH, DIM], F32R)
        w_lo = sb("w_lo", [P, 4, CH, DIM], F32R)
        b_qk = sb("b_qk", [P, 2, CH])
        bv = sb("bv", [P, DIM])
        bo = sb("bo", [P, DIM])
        x_tok = sb("x_tok", [P, TILES, DIM])
        xt_hi = sb("xt_hi", [P, CH, SEQ], F32R)
        xt_lo = sb("xt_lo", [P, CH, SEQ], F32R)
        parts = [sb(f"{n}_parts", [P, 3, CH, SEQ], BF16) for n in "qk"]
        rest = sb("rest", [P, 2 * CH, SEQ])
        qs = [sb(f"qs{i}", [P, HEADS, SEQ], BF16) for i in range(2)]
        ks = [sb(f"ks{i}", [P, HEADS, SEQ], BF16) for i in range(2)]
        vals = [sb(f"vals{i}", [P, TILES, HEADS, 32]) for i in range(2)]
        mx = sb("mx", [P, TILES, P])
        m_parts = sb("m_parts", [HEADS, 2, SEQ], BF16)
        probs = sb("probs", [P, 8, SEQ])
        ctx_t = sb("ctx_t", [P, GROUPS, SEQ])
        inv = sb("inv", [P, TILES, HEADS])
        ctx_tok = sb("ctx_tok", [P, TILES, DIM])
        ct_hi = sb("ct_hi", [P, CH, SEQ], F32R)
        ct_lo = sb("ct_lo", [P, CH, SEQ], F32R)
        x_res = sb("x_res", [P, TILES, DIM])
        res = sb("res", [P, TILES, DIM])
        stats = sb("stats", [P, TILES, 6])
        moments = sb("moments", [P, TILES, 2])
        rstd = sb("rstd", [P, TILES])
        power = sb("power", [P, TILES])
        normed = sb("normed", [P, TILES, DIM])

        ps_exp = [ps(f"ps_exp{i}", [P, SEQ]) for i in range(2)]
        ps_pv = ps("ps_pv", [P, SEQ])
        ps_max = [ps(f"ps_max{i}", [P, 2, SEQ]) for i in range(2)]
        ps_a = [ps_max[1][:, i, :] for i in range(2)]
        ps_w = ps("ps_w", [P, SEQ])

        const_in = sem("const_in")
        weight_in = sem("weight_in")
        weight_hi = sem("weight_hi")
        weight_lo = sem("weight_lo")
        cleared = sem("cleared")
        x_in = sem("x_in")
        xres_in = sem("xres_in")
        xres_ready = sem("xres_ready")
        a_full = sem("a_full")
        a_high = sem("a_high")
        a_read = sem("a_read")
        part_m = sem("part_m")
        part_l = [sem("q_part_l"), sem("k_part_l")]
        saved = [[sem(f"{n}{f}_saved") for f in range(CH)] for n in "qk"]
        landed = [sem(f"landed{f}") for f in range(CH)]
        max_full = sem("max_full")
        max_read = sem("max_read")
        nm_full = sem("nm_full")
        nm_high = sem("nm_high")
        nm_read = sem("nm_read")
        m_saved = sem("m_saved")
        m_landed = sem("m_landed")
        exp_full = sem("exp_full")
        exp_done = sem("exp_done")
        pv_done = sem("pv_done")
        ctx_kept = sem("ctx_kept")
        w_full = sem("w_full")
        w_part = sem("w_part")
        w_read = sem("w_read")
        ln_stats = sem("ln_stats")
        ln_moments = sem("ln_moments")
        pool_through = sem("pool_through")
        dve_through = sem("dve_through")
        power_set = sem("power_set")
        ln_rstd = sem("ln_rstd")
        ln_done = sem("ln_done")
        y_saved = sem("y_saved")

        x_view = io["L0_attn_inputs"].rearrange("b (t p) d -> b p t d", p=P)
        y_view = y1.rearrange("b (t p) d -> b p t d", p=P)
        weights = [io[f"L0_attn_W{n}"].rearrange("(c p) n -> p c n", p=P) for n in "qkvo"]
        n_const = 0

        block = ctx.enter_context(nc.Block())

        def slots(eng, slot):
            slot(-1, 1, True, False, False, False)
            slot(0, 0, True, True, False, False)
            with eng.Fori(0, (BATCH - 2) // 2) as pair:
                slot(Linear(pair, 2, 1), 1, True, True, True, True)
                slot(Linear(pair, 2, 2), 0, True, True, True, True)
            slot(BATCH - 1, 1, False, True, True, True)
            slot(BATCH, 0, False, False, True, True)


        @block.sync
        def _(sync):
            sync.dma_start(ident[:], io["identity"]).then_inc(const_in, 16)
            for i, n in enumerate("qk"):
                for c in range(CH):
                    sync.dma_start(b_qk[:, i, c:c + 1], io[f"L0_attn_b{n}"][c * P:(c + 1) * P].rearrange("(p a) -> p a", a=1)).then_inc(const_in, 16)
            for t, n in ((bv, "v"), (bo, "o")):
                sync.dma_start(t[:], io[f"L0_attn_b{n}"].partition_broadcast(P)).then_inc(const_in, 16)
            for i in range(2):
                sync.dma_start(qs[i][ROW_BIAS:ROW_BIAS + 3], io["rows"].bitcast(BF16)[3:6]).then_inc(const_in, 16)
                sync.dma_start(ks[i][ROW_BIAS:ROW_BIAS + 5], io["rows"].bitcast(BF16)[0:5]).then_inc(const_in, 16)
            for i in range(4):
                wait(sync, weight_lo, i)
                sync.dma_start(w_raw[:], weights[i]).then_inc(weight_in, 16)
            sync.dma_start(x_tok[:], x_view[0]).then_inc(x_in, 16)

            def slot(s, e, has_a, has_e, has_w, has_prev):
                a, w = s + 1, s - 1
                if has_w:
                    wait(sync, w_read, w * 8)
                    sync.dma_start(x_res[:], x_view[count(w)]).then_inc(xres_in, 16)
                if has_a:
                    for f in range(CH):
                        for k, dram in enumerate((q_parts_dram, k_parts_dram)):
                            sync.wait_ge(part_l[k], count(a * CH + f + 1))
                            wait(sync, landed[f], a * 192)
                            sync.dma_start(dram[:, f * P:(f + 1) * P].rearrange("t p n -> p t n"),
                                           parts[k][:, :, f, :]).then_inc(saved[k][f], 16)
                        for k, dram, stack, blocks in ((0, q_parts_dram, qs, Q_PARTS), (1, k_parts_dram, ks, K_PARTS)):
                            sync.wait_ge(saved[k][f], count(a * 16 + 16))
                            wait(sync, exp_full, (a - 1) * STEPS)
                            for r, part in enumerate(blocks):
                                sync.dma_start(stack[1 - e][r * HEAD_DIM:(r + 1) * HEAD_DIM, 8 * f:8 * f + 8, :],
                                               dram[part, f * P:(f + 1) * P].rearrange("(h r) n -> r h n", r=HEAD_DIM)
                                               ).then_inc(landed[f], 16)
                    wait(sync, a_full, a * 8 + 2)
                    sync.dma_start(x_tok[:], x_view[count(a + 1) % BATCH]).then_inc(x_in, 16)
                if has_w:
                    sync.wait_ge(ln_done, count(w + 1))
                    sync.dma_start(y_view[count(w)], normed[:]).then_inc(y_saved, 16)
                if has_a:
                    sync.wait_ge(nm_read, count(a + 1))
                    sync.dma_start(m_parts_dram, m_parts[:]).then_inc(m_saved, 16)
                    sync.wait_ge(m_saved, count(a * 16 + 16))
                    sync.dma_start(qs[1 - e][ROW_MAX:ROW_MAX + 2], m_parts_dram.rearrange("h p n -> p h n")).then_inc(m_landed, 16)

            slots(sync, slot)
            sync.wait_ge(y_saved, BATCH * 16)
            sync.wait_ge(x_in, 16 * (BATCH + 1))

        @block.tensor
        def _(pe):
            pe.wait_ge(const_in, 16 * 11)
            pe.wait_ge(cleared, 3)
            pe.wait_ge(weight_lo, 4)

            def three_products(out, pairs):
                n = len(pairs)
                for i, (l_hi, l_lo, r_hi, r_lo) in enumerate(pairs):
                    nc.tensor.matmul(out, l_hi, r_hi, start=i == 0, stop=False)
                    nc.tensor.matmul(out, l_hi, r_lo, start=False, stop=False)
                    last = nc.tensor.matmul(out, l_lo, r_hi, start=False, stop=i == n - 1)
                return last

            def scores_for_exp(b, e, u):
                tick, j = u // 4, u % 4
                head, kt = 4 * (tick // 4) + j, tick % 4
                if u == 0:
                    pe.wait_ge(m_landed, count(b * 16 + 16))
                wait(pe, exp_done, b * STEPS + u - 1)
                nc.tensor.matmul(ps_exp[u % 2][:], ks[e][0:ROWS_EXP, head, kt * P:(kt + 1) * P],
                                 qs[e][0:ROWS_EXP, head, :], start=True, stop=True).then_inc(exp_full, 1)

            def probs_times_values(b, e, tick):
                g, kt = tick // 4, tick % 4
                if tick == 0:
                    pe.wait_ge(a_read, count(b * 8 + 8))
                if kt == 0:
                    wait(pe, ctx_kept, b * GROUPS + g)
                pe.wait_ge(exp_done, count(b * STEPS + 4 * tick + 4))
                for j in range(4):
                    last = nc.tensor.matmul(ps_pv[32 * j:32 * j + 32, :], vals[e][:, kt, 4 * g + j, :],
                                            probs[:, 4 * (tick % 2) + j, :], start=kt == 0, stop=kt == 3)
                last.then_inc(pv_done, 1)

            def scores_for_max(a, e, n):
                head, half = n // 2, n % 2
                if n == 0:
                    wait(pe, nm_read, a)
                    pe.wait_ge(a_read, count(a * 8 + 8))
                if head % 8 == 0 and half == 0:
                    pe.wait_ge(landed[head // 8], count(a * 192 + 192))
                wait(pe, max_read, a * 32 + n - 1)
                for i in range(2):
                    qt = 2 * half + i
                    last = nc.tensor.matmul(ps_max[n % 2][:, i, :], qs[1 - e][0:ROWS_MAX, head, qt * P:(qt + 1) * P],
                                            ks[1 - e][0:ROWS_MAX, head, :], start=True, stop=True)
                last.then_inc(max_full, 1)

            def side(kind, i, a, w):
                if kind == "xt":
                    if i == 0:
                        pe.wait_ge(x_in, count(a * 16 + 16))
                        wait(pe, max_read, a * 32)
                    wait(pe, a_read, a * 8 + i - 1)
                    for t in range(TILES):
                        last = nc.tensor.transpose(ps_a[i][:, t * P:(t + 1) * P], x_tok[:, t, i * P:(i + 1) * P], ident[:])
                    last.then_inc(a_full, 1)
                if kind == "proj":
                    pe.wait_ge(a_read, count(a * 8 + 2 + max(i - 1, 0)))
                    k, f = i % 2, i // 2
                    three_products(ps_a[i % 2], [
                        (w_hi[:, k, c, f * P:(f + 1) * P], w_lo[:, k, c, f * P:(f + 1) * P], xt_hi[:, c], xt_lo[:, c])
                        for c in range(CH)]).then_inc(a_full, 1)
                if kind == "v":
                    pe.wait_ge(a_read, count(a * 8 + 5 + i))
                    for h in range(2):
                        t = slice((2 * i + h) * P, (2 * i + h + 1) * P)
                        last = three_products(ps_a[i][:, h * DIM:(h + 1) * DIM], [
                            (xt_hi[:, c, t], xt_lo[:, c, t], w_hi[:, 2, c], w_lo[:, 2, c]) for c in range(CH)])
                    last.then_inc(a_full, 1)
                if kind == "ct":
                    if i == 0:
                        pe.wait_ge(ctx_kept, count(w * GROUPS + GROUPS))
                        pe.wait_ge(nm_read, BATCH if isinstance(w, int) and w + 2 > BATCH else count(w + 2))
                    wait(pe, w_read, w * 8 + i)
                    for g in range(GROUPS):
                        last = nc.tensor.transpose(ps_w[:, g * P:(g + 1) * P], ctx_t[:, g, i * P:(i + 1) * P], ident[:])
                    last.then_inc(w_full, 1)
                if kind == "cb":
                    pe.wait_ge(w_read, count(w * 8 + 4 + i))
                    for t in range(TILES):
                        last = nc.tensor.transpose(ps_w[:, t * P:(t + 1) * P], ctx_tok[:, t, i * P:(i + 1) * P], ident[:])
                    last.then_inc(w_full, 1)
                if kind == "wo":
                    pe.wait_ge(w_read, count(w * 8 + 6 + i))
                    for h in range(2):
                        t = slice((2 * i + h) * P, (2 * i + h + 1) * P)
                        last = three_products(ps_w[:, h * DIM:(h + 1) * DIM], [
                            (ct_hi[:, c, t], ct_lo[:, c, t], w_hi[:, 3, c], w_lo[:, 3, c]) for c in range(CH)])
                    last.then_inc(w_full, 1)
                if kind == "nm":
                    pe.wait_ge(max_read, count(a * 32 + 32))
                    wait(pe, w_read, (w + 1) * 8)
                    for t in range(TILES):
                        last = nc.tensor.transpose(ps_w[:, t * P:(t + 1) * P], mx[:, t, :], ident[:])
                    last.then_inc(nm_full, 1)

            def slot(s, e, has_a, has_e, has_w, has_prev):
                for u in range(BEFORE, BEHIND + 1):
                    if has_e and 0 <= u < STEPS:
                        scores_for_exp(s, e, u)
                        if u % 4 == 1 and u >= 4:
                            probs_times_values(s, e, u // 4 - 1)
                    if has_a:
                        for n in maxima_of(u):
                            scores_for_max(s + 1, e, n)
                    for kind, i in SIDE.get(u, ()):
                        if kind == "pv":
                            if has_prev:
                                probs_times_values(s - 1, 1 - e, 15)
                        elif has_a if kind in INPUT_SIDE else has_w:
                            side(kind, i, s + 1, s - 1)

            slots(pe, slot)

        @block.scalar
        def _(act):
            act.wait_ge(const_in, 16 * 11)
            act.wait_ge(weight_hi, 5)

            def exponential(b, e, u):
                tick = u // 4
                if u % 4 == 0:
                    wait(act, pv_done, b * 16 + tick - 1)
                act.wait_ge(exp_full, count(b * STEPS + u + 1))
                nc.scalar.activation(probs[:, u % 8, :], ps_exp[u % 2][:], ACT.Exp).then_inc(exp_done, 1)

            def keep_context(b, g):
                act.wait_ge(pv_done, count(b * 16 + 4 * g + 4))
                if g == 0:
                    wait(act, w_full, b * 8 - 4)
                nc.scalar.activation(ctx_t[:, g, :], ps_pv[:], ACT.Copy).then_inc(ctx_kept, 1)

            def middle_part(a, i):
                act.wait_ge(a_read, count(a * 8 + 3 + i))
                nc.scalar.activation(parts[i % 2][:, 1, i // 2, :], rest[:, i], ACT.Copy).then_inc(part_m, 1)

            def side(kind, i, a, w):
                if kind == "xt":
                    act.wait_ge(a_full, count(a * 8 + i + 1))
                    nc.scalar.activation(xt_hi[:, i], ps_a[i], ACT.Copy).then_inc(a_high, 1)
                if kind == "proj":
                    act.wait_ge(a_full, count(a * 8 + 3 + i))
                    k, f = i % 2, i // 2
                    wait(act, saved[k][f], a * 16)
                    nc.scalar.activation(parts[k][:, 0, f, :], ps_a[i % 2], ACT.Identity,
                                         bias=b_qk[:, k, f:f + 1]).then_inc(a_high, 1)
                if kind == "cb":
                    act.wait_ge(w_full, count(w * 8 + 5 + i))
                    nc.scalar.activation(ct_hi[:, i], ps_w[:], ACT.Copy).then_inc(w_part, 1)

            def slot(s, e, has_a, has_e, has_w, has_prev):
                a = s + 1
                for u in range(BEFORE, BEHIND + 1):
                    if has_e and 0 <= u < STEPS:
                        exponential(s, e, u)
                        if u % 16 == 2 and u > 16:
                            keep_context(s, u // 16 - 1)
                    for kind, i in SIDE.get(u, ()):
                        if kind == "pv":
                            if has_prev:
                                keep_context(s - 1, GROUPS - 1)
                        elif (kind in ("xt", "proj") and has_a) or (kind == "cb" and has_w):
                            side(kind, i, s + 1, s - 1)
                            if kind == "proj" and i > 0:
                                middle_part(a, i - 1)
                            if kind == "proj" and i == 3:
                                middle_part(a, i)

            slots(act, slot)

        @block.vector
        def _(dve):
            nc.vector.memset(mx[:], 0.0).then_inc(cleared, 1)
            for i in range(2):
                nc.vector.memset(vals[i][:], 0.0).then_inc(cleared, 1)
            dve.wait_ge(cleared, 3)
            for i in range(2):
                nc.vector.memset(vals[i][:, :, :, HEAD_DIM:HEAD_DIM + 1], 1.0).then_inc(cleared, 1)
            dve.wait_ge(const_in, 16 * 11)
            for i in range(4):
                scale = QSCALE if i == 0 else 1.0
                dve.wait_ge(weight_in, 16 * i + 16)
                nc.vector.tensor_scalar(w_hi[:, i], w_raw[:], scale, None, ALU.mult).then_inc(weight_hi, 1)
                dve.wait_ge(weight_hi, i + 1)
                nc.vector.scalar_tensor_tensor(out=w_lo[:, i], in0=w_raw[:], scalar=scale, in1=w_hi[:, i].bitcast(F32),
                                               op0=ALU.mult, op1=ALU.subtract).then_inc(weight_lo, 1)
            nc.vector.tensor_scalar(b_qk[:, 0], b_qk[:, 0], QSCALE, None, ALU.mult).then_inc(weight_hi, 1)
            dve.wait_ge(weight_hi, 5)

            def row_max(a, n):
                head, half = n // 2, n % 2
                if n == 0:
                    wait(dve, nm_full, a)
                dve.wait_ge(max_full, count(a * 32 + n + 1))
                nc.vector.tensor_reduce(mx[:, 2 * half:2 * half + 2, head:head + 1], ps_max[n % 2][:], AX_X, ALU.max).then_inc(max_read, 1)

            def low_part(a, i):
                dve.wait_ge(part_m, count(a * 4 + i + 1))
                nc.vector.tensor_tensor(parts[i % 2][:, 2, i // 2, :], rest[:, i], parts[i % 2][:, 1, i // 2, :],
                                        ALU.subtract).then_inc(part_l[i % 2], 1)

            def side(kind, i, a, w, e):
                if kind == "xt":
                    dve.wait_ge(a_high, count(a * 6 + i + 1))
                    nc.vector.tensor_tensor(xt_lo[:, i], ps_a[i], xt_hi[:, i].bitcast(F32), ALU.subtract).then_inc(a_read, 1)
                if kind == "proj":
                    k, f = i % 2, i // 2
                    dve.wait_ge(a_high, count(a * 6 + 3 + i))
                    if k == 0:
                        wait(dve, part_l[0], a * CH + f - 1)
                    nc.vector.scalar_tensor_tensor(out=rest[:, i], in0=ps_a[i % 2], scalar=b_qk[:, k, f:f + 1],
                                                   in1=parts[k][:, 0, f, :], op0=ALU.add, op1=ALU.subtract).then_inc(a_read, 1)
                if kind == "v":
                    dve.wait_ge(a_full, count(a * 8 + 7 + i))
                    if i == 0:
                        wait(dve, pv_done, (a - 1) * 16)
                    nc.vector.tensor_tensor(
                        vals[1 - e][:, 2 * i:2 * i + 2, :, 0:HEAD_DIM],
                        ps_a[i].rearrange("p (t h d) -> p t h d", t=2, h=HEADS),
                        bv[:].rearrange("p (a h d) -> p a h d", a=1, h=HEADS).to_broadcast([P, 2, HEADS, HEAD_DIM]),
                        ALU.add).then_inc(a_read, 1)
                if kind == "ct":
                    dve.wait_ge(w_full, count(w * 8 + i + 1))
                    rows = ps_w[:].rearrange("p (h d) -> p h d", d=32)
                    nc.vector.reciprocal(inv[:, i, :].rearrange("p (h a) -> p h a", a=1), rows[:, :, HEAD_DIM:HEAD_DIM + 1]).then_inc(w_part, 1)
                    dve.wait_ge(w_part, count(w * 6 + i + 1))
                    nc.vector.tensor_tensor(
                        ctx_tok[:, i, :].rearrange("p (h d) -> p h d", d=HEAD_DIM), rows[:, :, 0:HEAD_DIM],
                        inv[:, i, :].rearrange("p (h a) -> p h a", a=1).to_broadcast([P, HEADS, HEAD_DIM]),
                        ALU.mult).then_inc(w_read, 1)
                if kind == "cb":
                    dve.wait_ge(w_part, count(w * 6 + 5 + i))
                    nc.vector.tensor_tensor(ct_lo[:, i], ps_w[:], ct_hi[:, i].bitcast(F32), ALU.subtract).then_inc(w_read, 1)
                if kind == "wo":
                    dve.wait_ge(w_full, count(w * 8 + 7 + i))
                    if i == 0:
                        dve.wait_ge(xres_ready, count(w + 1))
                        wait(dve, ln_done, w)
                    nc.vector.tensor_tensor(res[:, 2 * i:2 * i + 2, :], ps_w[:].rearrange("p (t d) -> p t d", t=2),
                                            x_res[:, 2 * i:2 * i + 2, :], ALU.add).then_inc(w_read, 1)
                if kind == "ln":
                    dve.wait_ge(w_read, count(w * 8 + 8))
                    for t in range(TILES):
                        nc.vector.bn_stats(stats[:, t, :], res[:, t, :]).then_inc(ln_stats, 1)
                    for t in range(TILES):
                        dve.wait_ge(ln_stats, count(w * TILES + t + 1))
                        dve.sem_inc(dve_through)
                        nc.vector.bn_aggr(moments[:, t, :], stats[:, t, :]).then_inc(ln_moments, 1)
                if kind == "norm":
                    dve.wait_ge(ln_rstd, count(w * 2 + 2))
                    wait(dve, y_saved, w * 16)
                    for t in range(TILES):
                        last = nc.vector.tensor_scalar(normed[:, t, :], res[:, t, :], moments[:, t, 0:1], rstd[:, t:t + 1],
                                                       ALU.subtract, ALU.mult)
                    last.then_inc(ln_done, 1)
                if kind == "nm":
                    dve.wait_ge(nm_full, count(a + 1))
                    wait(dve, m_saved, a * 16)
                    nc.vector.tensor_scalar(m_parts[:, 0, :], ps_w[0:HEADS, :], -1.0, None, ALU.mult).then_inc(nm_high, 1)
                    dve.wait_ge(nm_high, count(a + 1))
                    nc.vector.scalar_tensor_tensor(out=m_parts[:, 1, :], in0=ps_w[0:HEADS, :], scalar=-1.0, in1=m_parts[:, 0, :],
                                                   op0=ALU.mult, op1=ALU.subtract).then_inc(nm_read, 1)

            def slot(s, e, has_a, has_e, has_w, has_prev):
                a = s + 1
                for u in range(BEFORE, BEHIND + 1):
                    if has_a:
                        for n in maxima_of(u):
                            row_max(a, n)
                    for kind, i in SIDE.get(u, ()):
                        if kind != "pv" and (has_a if kind in INPUT_SIDE else has_w):
                            side(kind, i, a, s - 1, e)
                            if kind == "proj" and i == 2:
                                low_part(a, 1)
                            if kind == "proj" and i == 3:
                                low_part(a, 3)

            slots(dve, slot)

        @block.gpsimd
        def _(pool):
            nc.gpsimd.memset(power[:], -0.5).then_inc(power_set, 1)
            pool.wait_ge(const_in, 16 * 11)
            pool.wait_ge(power_set, 1)

            def slot(s, e, has_a, has_e, has_w, has_prev):
                a, w = s + 1, s - 1
                if has_w:
                    pool.wait_ge(xres_in, count(w * 16 + 16))
                    nc.gpsimd.tensor_tensor(x_res[:], x_res[:], bo[:].rearrange("p (a d) -> p a d", a=1).to_broadcast([P, TILES, DIM]),
                                            ALU.add).then_inc(xres_ready, 1)
                if has_a:
                    for f in range(CH):
                        pool.wait_ge(part_m, count(a * 4 + 2 * f + 1))
                        nc.gpsimd.tensor_tensor(parts[0][:, 2, f, :], rest[:, 2 * f], parts[0][:, 1, f, :],
                                                ALU.subtract).then_inc(part_l[0], 1)
                if has_w:
                    pool.wait_ge(ln_moments, count(w * TILES + TILES))
                    pool.sem_inc(pool_through)
                    nc.gpsimd.tensor_scalar(rstd[:].rearrange("p (t a) -> p t a", a=1), moments[:, :, 1:2], EPS, None, ALU.add).then_inc(ln_rstd, 1)
                    pool.wait_ge(ln_rstd, count(w * 2 + 1))
                    nc.gpsimd.tensor_tensor(rstd[:], rstd[:], power[:], ALU.pow).then_inc(ln_rstd, 1)

            slots(pool, slot)


def feed_forward(nc, io, y1, out):
    with ExitStack() as ctx:
        def sb(name, shape, dt=F32):
            return ctx.enter_context(nc.sbuf_tensor(name, shape, dt))

        def ps(name, shape):
            return ctx.enter_context(nc.psum_tensor(name, shape, F32))

        def sem(name):
            return ctx.enter_context(nc.semaphore(name))

        ident = sb("f_ident", [P, P])
        w_raw = sb("f_w_raw", [P, 2048])
        w1_hi = sb("w1_hi", [P, CH, HIDDEN], F32R)
        w1_lo = sb("w1_lo", [P, CH, HIDDEN], F32R)
        w2_hi = sb("w2_hi", [P, HC, DIM], F32R)
        w2_lo = sb("w2_lo", [P, HC, DIM], F32R)
        wr_raw = sb("wr_raw", [EXPERTS, DIM])
        wr_hi = sb("wr_hi", [P, CH, EXPERTS], F32R)
        wr_lo = sb("wr_lo", [P, CH, EXPERTS], F32R)
        b1 = sb("b1", [P, HC])
        b2 = sb("b2", [P, DIM])
        y = [sb(f"rows{i}", [P, TILES, DIM]) for i in range(2)]
        yt_hi = sb("yt_hi", [P, CH, SEQ], F32R)
        yt_lo = sb("yt_lo", [P, CH, SEQ], F32R)
        act_out = sb("act_out", [P, 4, SEQ])
        h_hi = [sb(f"h_hi{i}", [P, HC, SEQ], F32R) for i in range(2)]
        h_lo = [sb(f"h_lo{i}", [P, HC, SEQ], F32R) for i in range(2)]
        top = sb("top", [P, TILES])
        shifted = sb("shifted", [P, TILES, EXPERTS])
        expd = sb("expd", [P, TILES, EXPERTS])
        total = sb("total", [P, TILES])
        inv = sb("f_inv", [P, TILES])
        gate = [sb(f"gate{i}", [P, TILES]) for i in range(2)]
        ffn = sb("ffn", [P, TILES, DIM])
        res = sb("f_res", [P, TILES, DIM])
        stats = sb("f_stats", [P, TILES, 6])
        moments = sb("f_moments", [P, TILES, 2])
        rstd = sb("f_rstd", [P, TILES])
        power = sb("f_power", [P, TILES])
        normed = sb("f_normed", [P, TILES, DIM])

        ps_t = [ps(f"ps_t{i}", [P, SEQ]) for i in range(2)]
        ps_r = ps("ps_r", [P, TILES, EXPERTS])
        ps_1 = [ps(f"ps_1{i}", [P, SEQ]) for i in range(2)]
        ps_2 = [ps(f"ps_2{i}", [P, 2, DIM]) for i in range(2)]

        const_in = sem("f_const_in")
        weight_in = sem("f_weight_in")
        weight_hi = sem("f_weight_hi")
        weight_lo = sem("f_weight_lo")
        wr_turned = sem("wr_turned")
        y_in = sem("y_in")
        t_full = sem("t_full")
        t_high = sem("t_high")
        t_read = sem("t_read")
        r_full = sem("r_full")
        r_step = sem("r_step")
        r_exp = sem("r_exp")
        f1_full = sem("f1_full")
        f1_act = sem("f1_act")
        h_high = sem("h_high")
        h_low = [sem(f"h_low{i}") for i in range(2)]
        f2_full = sem("f2_full")
        f2_read = sem("f2_read")
        gated = sem("gated")
        ln_stats = sem("f_ln_stats")
        ln_moments = sem("f_ln_moments")
        pool_through = sem("f_pool_through")
        dve_through = sem("f_dve_through")
        power_set = sem("f_power_set")
        ln_rstd = sem("f_ln_rstd")
        ln_done = sem("f_ln_done")
        out_saved = sem("out_saved")

        y_view = y1.rearrange("b (t p) d -> b p t d", p=P)
        out_view = out.rearrange("b (t p) d -> b p t d", p=P)
        last_expert = EXPERTS - 1
        w1_view = io["L0_ffn_W1"][last_expert].rearrange("(c p) f -> p c f", p=P)
        w2_view = io["L0_ffn_W2"][last_expert].rearrange("(c p) n -> p c n", p=P)
        w_flat = w_raw[:]

        block = ctx.enter_context(nc.Block())

        def slots(eng, slot):
            slot(-1, 1, True, False)
            slot(0, 0, True, True)
            with eng.Fori(0, (BATCH - 2) // 2) as pair:
                slot(Linear(pair, 2, 1), 1, True, True)
                slot(Linear(pair, 2, 2), 0, True, True)
            slot(BATCH - 1, 1, False, True)


        @block.sync
        def _(sync):
            sync.dma_start(y[0][:], y_view[0]).then_inc(y_in, 16)
            sync.dma_start(w_raw[:].rearrange("p (c f) -> p c f", c=CH), w1_view).then_inc(weight_in, 16)
            sync.dma_start(ident[:], io["identity"]).then_inc(const_in, 16)
            sync.dma_start(wr_raw[:], io["L0_ffn_Wr"]).then_inc(const_in, 16)
            for c in range(HC):
                sync.dma_start(b1[:, c:c + 1], io["L0_ffn_b1"][last_expert, c * P:(c + 1) * P].rearrange("(p a) -> p a", a=1)).then_inc(const_in, 16)
            sync.dma_start(b2[:], io["L0_ffn_b2"][last_expert].partition_broadcast(P)).then_inc(const_in, 16)
            sync.wait_ge(weight_lo, 1)
            sync.dma_start(w_raw[:].rearrange("p (c n) -> p c n", c=HC), w2_view).then_inc(weight_in, 16)

            def slot(s, e, has_n, has_f):
                if has_n:
                    if has_f:
                        sync.wait_ge(gated, count(s * TILES + TILES))
                    sync.dma_start(y[e][:], y_view[count(s + 2) % BATCH]).then_inc(y_in, 16)
                if has_f:
                    sync.wait_ge(ln_done, count(s + 1))
                    sync.dma_start(out_view[count(s)], normed[:]).then_inc(out_saved, 16)

            slots(sync, slot)
            sync.wait_ge(out_saved, BATCH * 16)

        @block.tensor
        def _(pe):
            pe.wait_ge(const_in, 16 * 11)
            for c in range(CH):
                last = nc.tensor.transpose(ps_r[:].rearrange("p t x -> p (t x)")[:, c * EXPERTS:(c + 1) * EXPERTS],
                                           wr_raw[:, c * P:(c + 1) * P], ident[0:EXPERTS, 0:EXPERTS])
            last.then_inc(wr_turned, 1)
            pe.wait_ge(weight_lo, 3)

            def turn_rows(n, e, c):
                if c == 0:
                    pe.wait_ge(y_in, count(n * 16 + 16))
                wait(pe, t_read, n * 2 + c - 1)
                for t in range(TILES):
                    last = nc.tensor.transpose(ps_t[c][:, t * P:(t + 1) * P], y[1 - e][:, t, c * P:(c + 1) * P], ident[:])
                last.then_inc(t_full, 1)

            def router(n):
                pe.wait_ge(t_read, count(n * 2 + 2))
                wait(pe, r_step, n * 5 - 3)
                for t in range(TILES):
                    i = 0
                    for c in range(CH):
                        ts = slice(t * P, (t + 1) * P)
                        for l, r in ((yt_hi, wr_hi), (yt_hi, wr_lo), (yt_lo, wr_hi)):
                            last = nc.tensor.matmul(ps_r[:, t, :], l[:, c, ts], r[:, c, :], start=i == 0, stop=i == 5)
                            i += 1
                last.then_inc(r_full, 1)

            def first_product(n, i):
                wait(pe, f1_act, n * HC + i - 1)
                k = 0
                for c in range(CH):
                    for l, r in ((w1_hi, yt_hi), (w1_hi, yt_lo), (w1_lo, yt_hi)):
                        last = nc.tensor.matmul(ps_1[i % 2][:], l[:, c, i * P:(i + 1) * P], r[:, c, :], start=k == 0, stop=k == 5)
                        k += 1
                last.then_inc(f1_full, 1)

            def second_product(s, e, i):
                t = i // 2
                ts = slice(t * P, (t + 1) * P)
                if i == 0:
                    pe.wait_ge(h_low[0], count(s * 4 + 4))
                    pe.wait_ge(h_low[1], count(s * 4 + 4))
                if i % 2 == 0:
                    wait(pe, f2_read, s * TILES + t - 1)
                for c in range(4 * (i % 2), 4 * (i % 2) + 4):
                    for l, r in ((h_hi, w2_hi), (h_hi, w2_lo), (h_lo, w2_hi)):
                        last = nc.tensor.matmul(ps_2[t % 2][:, t // 2, :], l[e][:, c, ts], r[:, c, :],
                                                start=c == 0 and l is h_hi and r is w2_hi, stop=c == HC - 1 and l is h_lo)
                if i % 2:
                    last.then_inc(f2_full, 1)

            def slot(s, e, has_n, has_f):
                if has_n:
                    turn_rows(s + 1, e, 0)
                    turn_rows(s + 1, e, 1)
                if has_f:
                    second_product(s, e, 0)
                    second_product(s, e, 1)
                if has_n:
                    router(s + 1)
                for i in range(HC):
                    if has_n:
                        first_product(s + 1, i)
                    if has_f and i < HC - 2:
                        second_product(s, e, i + 2)

            slots(pe, slot)

        @block.scalar
        def _(act):
            act.wait_ge(const_in, 16 * 11)

            def slot(s, e, has_n, has_f):
                n = s + 1
                if not has_n:
                    return
                for c in range(CH):
                    act.wait_ge(t_full, count(n * 2 + c + 1))
                    nc.scalar.activation(yt_hi[:, c], ps_t[c][:], ACT.Copy).then_inc(t_high, 1)
                act.wait_ge(r_step, count(n * 5 + 2))
                nc.scalar.activation(expd[:], shifted[:], ACT.Exp).then_inc(r_exp, 1)
                for i in range(HC):
                    act.wait_ge(f1_full, count(n * HC + i + 1))
                    wait(act, h_low[i % 2], n * 4 + i // 2 - 1)
                    nc.scalar.activation(act_out[:, i % 4, :], ps_1[i % 2][:], ACT.Gelu, bias=b1[:, i:i + 1]).then_inc(f1_act, 1)

            slots(act, slot)

        @block.vector
        def _(dve):
            dve.wait_ge(const_in, 16 * 11)
            for i, (hi, lo) in enumerate(((w1_hi, w1_lo), (w2_hi, w2_lo))):
                dve.wait_ge(weight_in, 16 * i + 16)
                src = w_flat.rearrange("p (c n) -> p c n", c=(CH, HC)[i])
                nc.vector.tensor_copy(hi[:], src).then_inc(weight_hi, 1)
                dve.wait_ge(weight_hi, i + 1)
                nc.vector.tensor_tensor(lo[:], src, hi[:].bitcast(F32), ALU.subtract).then_inc(weight_lo, 1)
            dve.wait_ge(wr_turned, 1)
            turned = ps_r[:].rearrange("p t x -> p (t x)")[:, 0:CH * EXPERTS].rearrange("p (c x) -> p c x", c=CH)
            nc.vector.tensor_copy(wr_hi[:], turned).then_inc(weight_hi, 1)
            dve.wait_ge(weight_hi, 3)
            nc.vector.tensor_tensor(wr_lo[:], turned, wr_hi[:].bitcast(F32), ALU.subtract).then_inc(weight_lo, 1)

            def column(x):
                return x.rearrange("p (t a) -> p t a", a=1)

            def epilogue(s, e, t):
                dve.wait_ge(f2_full, count(s * TILES + t + 1))
                nc.vector.tensor_tensor(ffn[:, t, :], ps_2[t % 2][:, t // 2, :], b2[:], ALU.add).then_inc(f2_read, 1)
                dve.wait_ge(f2_read, count(s * TILES + t + 1))
                wait(dve, ln_done, s)
                nc.vector.scalar_tensor_tensor(out=res[:, t, :], in0=ffn[:, t, :], scalar=gate[e][:, t:t + 1], in1=y[e][:, t, :],
                                               op0=ALU.mult, op1=ALU.add).then_inc(gated, 1)
                dve.wait_ge(gated, count(s * TILES + t + 1))
                nc.vector.bn_stats(stats[:, t, :], res[:, t, :]).then_inc(ln_stats, 1)
                dve.wait_ge(ln_stats, count(s * TILES + t + 1))
                dve.sem_inc(dve_through)
                nc.vector.bn_aggr(moments[:, t, :], stats[:, t, :]).then_inc(ln_moments, 1)

            def slot(s, e, has_n, has_f):
                n = s + 1
                if has_n:
                    for c in range(CH):
                        dve.wait_ge(t_high, count(n * 2 + c + 1))
                        nc.vector.tensor_tensor(yt_lo[:, c], ps_t[c][:], yt_hi[:, c].bitcast(F32), ALU.subtract).then_inc(t_read, 1)
                if has_f:
                    epilogue(s, e, 0)
                if has_n:
                    dve.wait_ge(r_full, count(n + 1))
                    nc.vector.tensor_reduce(top[:], ps_r[:], AX_X, ALU.max).then_inc(r_step, 1)
                    dve.wait_ge(r_step, count(n * 5 + 1))
                    nc.vector.tensor_tensor(shifted[:], ps_r[:], column(top[:]).to_broadcast([P, TILES, EXPERTS]),
                                            ALU.subtract).then_inc(r_step, 1)
                for i in range(HC):
                    if has_n:
                        dve.wait_ge(f1_act, count(n * HC + i + 1))
                        nc.vector.tensor_copy(h_hi[1 - e][:, i, :], act_out[:, i % 4, :]).then_inc(h_high, 1)
                        if i % 2:
                            dve.wait_ge(h_high, count(n * HC + i + 1))
                            nc.vector.tensor_tensor(h_lo[1 - e][:, i, :], act_out[:, i % 4, :], h_hi[1 - e][:, i, :].bitcast(F32),
                                                    ALU.subtract).then_inc(h_low[1], 1)
                    if has_n and i == 0:
                        dve.wait_ge(r_exp, count(n + 1))
                        nc.vector.tensor_reduce(total[:], expd[:], AX_X, ALU.add).then_inc(r_step, 1)
                        dve.wait_ge(r_step, count(n * 5 + 3))
                        nc.vector.reciprocal(inv[:], total[:]).then_inc(r_step, 1)
                        dve.wait_ge(r_step, count(n * 5 + 4))
                        nc.vector.tensor_tensor(column(gate[1 - e][:]), expd[:, :, last_expert:EXPERTS], column(inv[:]),
                                                ALU.mult).then_inc(r_step, 1)
                    if has_f and i % 2 and i < 6:
                        epilogue(s, e, (i + 1) // 2)
                if has_f:
                    dve.wait_ge(ln_rstd, count(s * 2 + 2))
                    wait(dve, out_saved, s * 16)
                    for t in range(TILES):
                        last = nc.vector.tensor_scalar(normed[:, t, :], res[:, t, :], moments[:, t, 0:1], rstd[:, t:t + 1],
                                                       ALU.subtract, ALU.mult)
                    last.then_inc(ln_done, 1)

            slots(dve, slot)

        @block.gpsimd
        def _(pool):
            nc.gpsimd.memset(power[:], -0.5).then_inc(power_set, 1)
            pool.wait_ge(const_in, 16 * 11)
            pool.wait_ge(power_set, 1)

            def slot(s, e, has_n, has_f):
                n = s + 1
                if has_n:
                    for i in range(0, HC, 2):
                        pool.wait_ge(h_high, count(n * HC + i + 1))
                        nc.gpsimd.tensor_tensor(h_lo[1 - e][:, i, :], act_out[:, i % 4, :], h_hi[1 - e][:, i, :].bitcast(F32),
                                                ALU.subtract).then_inc(h_low[0], 1)
                if has_f:
                    pool.wait_ge(ln_moments, count(s * TILES + TILES))
                    pool.sem_inc(pool_through)
                    nc.gpsimd.tensor_scalar(rstd[:].rearrange("p (t a) -> p t a", a=1), moments[:, :, 1:2], EPS, None, ALU.add).then_inc(ln_rstd, 1)
                    pool.wait_ge(ln_rstd, count(s * 2 + 1))
                    nc.gpsimd.tensor_tensor(rstd[:], rstd[:], power[:], ALU.pow).then_inc(ln_rstd, 1)

            slots(pool, slot)


def build(nc, io, out):
    y1 = nc.dram_tensor("attn_out", [BATCH, SEQ, DIM], F32, kind="Internal").ap()
    q_parts = nc.dram_tensor("q_parts_dram", [3, DIM, SEQ], BF16, kind="Internal").ap()
    k_parts = nc.dram_tensor("k_parts_dram", [3, DIM, SEQ], BF16, kind="Internal").ap()
    m_parts = nc.dram_tensor("m_parts_dram", [HEADS, 2, SEQ], BF16, kind="Internal").ap()
    attention(nc, io, y1, q_parts, k_parts, m_parts)
    feed_forward(nc, io, y1, out)


_INS = ['L0_attn_inputs', 'L0_attn_Wq', 'L0_attn_bq', 'L0_attn_Wk', 'L0_attn_bk', 'L0_attn_Wv', 'L0_attn_bv',
        'L0_attn_Wo', 'L0_attn_bo', 'L0_ffn_Wr', 'L0_ffn_W1', 'L0_ffn_b1', 'L0_ffn_W2', 'L0_ffn_b2']


def constants():
    import numpy as np

    base = (2.0 ** 8) ** (1.0 / HEADS)
    slopes = np.asarray([1.0 / base ** (i + 1) for i in range(HEADS)], np.float32)
    bias = slopes[:, None] * np.arange(SEQ, dtype=np.float32)[None, :]
    rows = np.full((6, HEADS, SEQ), 0x3F80, np.uint16)
    for r in range(3):
        upper = bias.view(np.uint32) & np.uint32(0xFFFF0000)
        rows[r] = upper >> 16
        bias = bias - upper.view(np.float32)
    return {"identity": np.eye(P, dtype=np.float32), "rows": rows}


def kernel(**inputs):
    import numpy as np
    import concourse.bacc as bacc
    from concourse.bass_utils import run_bass_kernel_spmd

    nc = bacc.Bacc("TRN2", target_bir_lowering=False, num_devices=1)
    nc.disable_value_cache = True
    arrays, io = {}, {}
    for name, a in [(n, inputs[n]) for n in _INS] + list(constants().items()):
        a = np.ascontiguousarray(a)
        arrays[f"in_{name}"] = a
        io[name] = nc.dram_tensor(f"in_{name}", a.shape, mybir.dt.from_np(a.dtype), kind="ExternalInput").ap()
    out = nc.dram_tensor("out", (BATCH, SEQ, DIM), F32, kind="ExternalOutput").ap()
    build(nc, io, out)
    r = run_bass_kernel_spmd(nc, [arrays], core_ids=[0])
    return r.results[0]["out"]
```

```python
from contextlib import ExitStack

import concourse.bass as bass
from concourse import mybir

F32 = mybir.dt.float32
F32R = mybir.dt.float32r
BF16 = mybir.dt.bfloat16
ALU = mybir.AluOpType
ACT = mybir.ActivationFunctionType
AX_X = mybir.AxisListType.X

P = 128
BATCH, SEQ, DIM = 16, 512, 256
HEADS, HEAD_DIM = 16, 16
TILES = SEQ // P
CH = DIM // P
GROUPS = HEADS // 4
EXPERTS, HIDDEN = 8, 1024
HC = HIDDEN // P
EPS = 1e-5
QSCALE = HEAD_DIM ** -0.5

Q_PARTS = (0, 1, 2, 0, 1, 0)
K_PARTS = (2, 1, 0, 1, 0, 0)
Q_RUNS = ((3, 2, 0), (5, 1, 0), (0, 3, 0))
K_RUNS = ((3, 2, 1), (5, 1, 2), (0, 3, 0))
ROW_BIAS = len(Q_PARTS) * HEAD_DIM
ROW_MAX = ROW_BIAS + 3
ROWS_MAX = ROW_MAX
ROWS_EXP = ROW_MAX + 2

STEPS = 64

BEFORE, BEHIND = -1, STEPS
SIDE = {BEFORE: [("xt", 0), ("xt", 1), ("pv", 0), ("proj", 0), ("proj", 1), ("ct", 0)],
        0: [("proj", 2)], 1: [("ct", 1)], 2: [("proj", 3)], 3: [("ct", 2)], 4: [("v", 0)], 5: [("ct", 3)], 6: [("v", 1)],
        7: [("cb", 0)], 9: [("cb", 1)], 11: [("wo", 0)], 13: [("wo", 1)], 15: [("ln", 0)], 18: [("norm", 0)],
        63: [("nm", 0)]}
INPUT_SIDE = ("xt", "proj", "v", "nm")
MAX_FROM, MAX_TO = 13, 60


def maxima_of(u):
    if not MAX_FROM <= u < MAX_TO:
        return range(0)
    n, span = HEADS * TILES // 2, MAX_TO - MAX_FROM
    return range(n * (u - MAX_FROM) // span, n * (u - MAX_FROM + 1) // span)


class Linear:

    def __init__(self, pair, step, start):
        self.pair, self.step, self.start = pair, step, start

    def __add__(self, n):
        return Linear(self.pair, self.step, self.start + n)

    def __sub__(self, n):
        return self + -n

    def __mul__(self, n):
        return Linear(self.pair, self.step * n, self.start * n)


def count(x):
    return x.pair * x.step + x.start if isinstance(x, Linear) else x


def wait(eng, semaphore, x):
    if isinstance(x, Linear) or x > 0:
        eng.wait_ge(semaphore, count(x))


def attention(nc, io, y1, q_parts_dram, k_parts_dram, m_parts_dram):
    with ExitStack() as ctx:
        def sb(name, shape, dt=F32):
            return ctx.enter_context(nc.sbuf_tensor(name, shape, dt))

        def ps(name, shape):
            return ctx.enter_context(nc.psum_tensor(name, shape, F32))

        def sem(name):
            return ctx.enter_context(nc.semaphore(name))

        ident = sb("ident", [P, P])
        w_raw = sb("w_raw", [P, CH, DIM])
        w_hi = sb("w_hi", [P, 4, CH, DIM], F32R)
        w_lo = sb("w_lo", [P, 4, CH, DIM], F32R)
        b_qk = sb("b_qk", [P, 2, CH])
        bv = sb("bv", [P, DIM])
        bo = sb("bo", [P, DIM])
        x_tok = sb("x_tok", [P, TILES, DIM])
        xt_hi = sb("xt_hi", [P, CH, SEQ], F32R)
        xt_lo = sb("xt_lo", [P, CH, SEQ], F32R)
        parts = [sb(f"{n}_parts", [P, 3, CH, SEQ], BF16) for n in "qk"]
        rest = sb("rest", [P, 2 * CH, SEQ])
        qs = [sb(f"qs{i}", [P, HEADS, SEQ], BF16) for i in range(2)]
        ks = [sb(f"ks{i}", [P, HEADS, SEQ], BF16) for i in range(2)]
        vals = [sb(f"vals{i}", [P, TILES, HEADS, 32]) for i in range(2)]
        mx = sb("mx", [P, TILES, P])
        m_parts = sb("m_parts", [HEADS, 2, SEQ], BF16)
        probs = sb("probs", [P, 8, SEQ])
        ctx_t = sb("ctx_t", [P, GROUPS, SEQ])
        inv = sb("inv", [P, TILES, HEADS])
        ctx_tok = sb("ctx_tok", [P, TILES, DIM])
        ct_hi = sb("ct_hi", [P, CH, SEQ], F32R)
        ct_lo = sb("ct_lo", [P, CH, SEQ], F32R)
        x_res = sb("x_res", [P, TILES, DIM])
        res = sb("res", [P, TILES, DIM])
        stats = sb("stats", [P, TILES, 6])
        moments = sb("moments", [P, TILES, 2])
        rstd = sb("rstd", [P, TILES])
        power = sb("power", [P, TILES])
        normed = sb("normed", [P, TILES, DIM])

        ps_exp = [ps(f"ps_exp{i}", [P, SEQ]) for i in range(2)]
        ps_pv = ps("ps_pv", [P, SEQ])
        ps_max = [ps(f"ps_max{i}", [P, 2, SEQ]) for i in range(2)]
        ps_a = [ps_max[1][:, i, :] for i in range(2)]
        ps_w = ps("ps_w", [P, SEQ])

        const_in = sem("const_in")
        weight_in = sem("weight_in")
        weight_hi = sem("weight_hi")
        weight_lo = sem("weight_lo")
        cleared = sem("cleared")
        x_in = sem("x_in")
        xres_in = sem("xres_in")
        xres_ready = sem("xres_ready")
        a_full = sem("a_full")
        a_high = sem("a_high")
        a_read = sem("a_read")
        part_m = sem("part_m")
        part_l = [sem("q_part_l"), sem("k_part_l")]
        saved = [[sem(f"{n}{f}_saved") for f in range(CH)] for n in "qk"]
        landed = [sem(f"landed{f}") for f in range(CH)]
        max_full = sem("max_full")
        max_read = sem("max_read")
        nm_full = sem("nm_full")
        nm_high = sem("nm_high")
        nm_read = sem("nm_read")
        m_saved = sem("m_saved")
        m_landed = sem("m_landed")
        exp_full = sem("exp_full")
        exp_done = sem("exp_done")
        pv_done = sem("pv_done")
        ctx_kept = sem("ctx_kept")
        w_full = sem("w_full")
        w_part = sem("w_part")
        w_read = sem("w_read")
        ln_stats = sem("ln_stats")
        ln_moments = sem("ln_moments")
        pool_through = sem("pool_through")
        dve_through = sem("dve_through")
        power_set = sem("power_set")
        ln_rstd = sem("ln_rstd")
        ln_done = sem("ln_done")
        y_saved = sem("y_saved")

        x_view = io["L0_attn_inputs"].rearrange("b (t p) d -> b p t d", p=P)
        y_view = y1.rearrange("b (t p) d -> b p t d", p=P)
        weights = [io[f"L0_attn_W{n}"].rearrange("(c p) n -> p c n", p=P) for n in "qkvo"]

        block = ctx.enter_context(nc.Block())

        def slots(eng, slot):
            slot(-1, 1, True, False, False, False)
            slot(0, 0, True, True, False, False)
            with eng.Fori(0, (BATCH - 2) // 2) as pair:
                slot(Linear(pair, 2, 1), 1, True, True, True, True)
                slot(Linear(pair, 2, 2), 0, True, True, True, True)
            slot(BATCH - 1, 1, False, True, True, True)
            slot(BATCH, 0, False, False, True, True)


        @block.sync
        def _(sync):
            sync.dma_start(ident[:], io["identity"]).then_inc(const_in, 16)
            for i, n in enumerate("qk"):
                for c in range(CH):
                    sync.dma_start(b_qk[:, i, c:c + 1], io[f"L0_attn_b{n}"][c * P:(c + 1) * P].rearrange("(p a) -> p a", a=1)).then_inc(const_in, 16)
            for t, n in ((bv, "v"), (bo, "o")):
                sync.dma_start(t[:], io[f"L0_attn_b{n}"].partition_broadcast(P)).then_inc(const_in, 16)
            for i in range(2):
                sync.dma_start(qs[i][ROW_BIAS:ROW_BIAS + 3], io["rows"].bitcast(BF16)[3:6]).then_inc(const_in, 16)
                sync.dma_start(ks[i][ROW_BIAS:ROW_BIAS + 5], io["rows"].bitcast(BF16)[0:5]).then_inc(const_in, 16)
            for i in range(4):
                wait(sync, weight_lo, i)
                sync.dma_start(w_raw[:], weights[i]).then_inc(weight_in, 16)
            sync.dma_start(x_tok[:], x_view[0]).then_inc(x_in, 16)

            def slot(s, e, has_a, has_e, has_w, has_prev):
                a, w = s + 1, s - 1
                if has_w:
                    wait(sync, w_read, w * 8)
                    sync.dma_start(x_res[:], x_view[count(w)]).then_inc(xres_in, 16)
                if has_a:
                    for f in range(CH):
                        wait(sync, landed[f], a * 96)
                        for part in range(3):
                            for k, dram in enumerate((q_parts_dram, k_parts_dram)):
                                if part == 0:
                                    sync.wait_ge(a_high, count(a * 6 + 3 + 2 * f + k))
                                elif part == 1:
                                    sync.wait_ge(part_m, count(a * 4 + 2 * f + k + 1))
                                else:
                                    sync.wait_ge(part_l[k], count(a * CH + f + 1))
                                sync.dma_start(dram[8 * f:8 * f + 8, 2 - part if k else part],
                                               parts[k][:, part, f, :]).then_inc(saved[k][f], 16)
                            if part == 0:
                                wait(sync, exp_full, (a - 1) * STEPS)
                                continue
                            for k, dram, stack, runs in ((0, q_parts_dram, qs, Q_RUNS), (1, k_parts_dram, ks, K_RUNS)):
                                sync.wait_ge(saved[k][f], count(a * 48 + 16 * (part + 1)))
                                for block, blocks, stored in (runs[0:2], runs[2:3])[part - 1]:
                                    sync.dma_start(
                                        stack[1 - e][block * HEAD_DIM:(block + blocks) * HEAD_DIM, 8 * f:8 * f + 8, :],
                                        dram[8 * f:8 * f + 8, stored:stored + blocks].rearrange("h t r n -> (t r) h n")
                                        ).then_inc(landed[f], 16)
                    wait(sync, a_full, a * 8 + 2)
                    sync.dma_start(x_tok[:], x_view[count(a + 1) % BATCH]).then_inc(x_in, 16)
                if has_w:
                    sync.wait_ge(ln_done, count(w + 1))
                    sync.dma_start(y_view[count(w)], normed[:]).then_inc(y_saved, 16)
                if has_a:
                    sync.wait_ge(nm_read, count(a + 1))
                    sync.dma_start(m_parts_dram, m_parts[:]).then_inc(m_saved, 16)
                    sync.wait_ge(m_saved, count(a * 16 + 16))
                    sync.dma_start(qs[1 - e][ROW_MAX:ROW_MAX + 2], m_parts_dram.rearrange("h p n -> p h n")).then_inc(m_landed, 16)

            slots(sync, slot)
            sync.wait_ge(y_saved, BATCH * 16)
            sync.wait_ge(x_in, 16 * (BATCH + 1))

        @block.tensor
        def _(pe):
            pe.wait_ge(const_in, 16 * 11)
            pe.wait_ge(cleared, 3)
            pe.wait_ge(weight_lo, 4)

            def three_products(out, pairs):
                n = len(pairs)
                for i, (l_hi, l_lo, r_hi, r_lo) in enumerate(pairs):
                    nc.tensor.matmul(out, l_hi, r_hi, start=i == 0, stop=False)
                    nc.tensor.matmul(out, l_hi, r_lo, start=False, stop=False)
                    last = nc.tensor.matmul(out, l_lo, r_hi, start=False, stop=i == n - 1)
                return last

            def scores_for_exp(b, e, u):
                tick, j = u // 4, u % 4
                head, kt = 4 * (tick // 4) + j, tick % 4
                if u == 0:
                    pe.wait_ge(m_landed, count(b * 16 + 16))
                wait(pe, exp_done, b * STEPS + u - 1)
                nc.tensor.matmul(ps_exp[u % 2][:], ks[e][0:ROWS_EXP, head, kt * P:(kt + 1) * P],
                                 qs[e][0:ROWS_EXP, head, :], start=True, stop=True).then_inc(exp_full, 1)

            def probs_times_values(b, e, tick):
                g, kt = tick // 4, tick % 4
                if tick == 0:
                    pe.wait_ge(a_read, count(b * 8 + 8))
                if kt == 0:
                    wait(pe, ctx_kept, b * GROUPS + g)
                pe.wait_ge(exp_done, count(b * STEPS + 4 * tick + 4))
                for j in range(4):
                    last = nc.tensor.matmul(ps_pv[32 * j:32 * j + 32, :], vals[e][:, kt, 4 * g + j, :],
                                            probs[:, 4 * (tick % 2) + j, :], start=kt == 0, stop=kt == 3)
                last.then_inc(pv_done, 1)

            def scores_for_max(a, e, n):
                head, half = n // 2, n % 2
                if n == 0:
                    pe.wait_ge(a_read, count(a * 8 + 8))
                if head % 8 == 0 and half == 0:
                    pe.wait_ge(landed[head // 8], count(a * 96 + 96))
                wait(pe, max_read, a * 32 + n - 1)
                for i in range(2):
                    qt = 2 * half + i
                    last = nc.tensor.matmul(ps_max[n % 2][:, i, :], qs[1 - e][0:ROWS_MAX, head, qt * P:(qt + 1) * P],
                                            ks[1 - e][0:ROWS_MAX, head, :], start=True, stop=True)
                last.then_inc(max_full, 1)

            def side(kind, i, a, w):
                if kind == "xt":
                    if i == 0:
                        pe.wait_ge(x_in, count(a * 16 + 16))
                        wait(pe, max_read, a * 32)
                    wait(pe, a_read, a * 8 + i - 1)
                    for t in range(TILES):
                        last = nc.tensor.transpose(ps_a[i][:, t * P:(t + 1) * P], x_tok[:, t, i * P:(i + 1) * P], ident[:])
                    last.then_inc(a_full, 1)
                if kind == "proj":
                    pe.wait_ge(a_read, count(a * 8 + 2 + max(i - 1, 0)))
                    k, f = i % 2, i // 2
                    three_products(ps_a[i % 2], [
                        (w_hi[:, k, c, f * P:(f + 1) * P], w_lo[:, k, c, f * P:(f + 1) * P], xt_hi[:, c], xt_lo[:, c])
                        for c in range(CH)]).then_inc(a_full, 1)
                if kind == "v":
                    pe.wait_ge(a_read, count(a * 8 + 5 + i))
                    for h in range(2):
                        t = slice((2 * i + h) * P, (2 * i + h + 1) * P)
                        last = three_products(ps_a[i][:, h * DIM:(h + 1) * DIM], [
                            (xt_hi[:, c, t], xt_lo[:, c, t], w_hi[:, 2, c], w_lo[:, 2, c]) for c in range(CH)])
                    last.then_inc(a_full, 1)
                if kind == "ct":
                    if i == 0:
                        pe.wait_ge(ctx_kept, count(w * GROUPS + GROUPS))
                        pe.wait_ge(nm_read, BATCH if isinstance(w, int) and w + 2 > BATCH else count(w + 2))
                    wait(pe, w_read, w * 8 + i)
                    for g in range(GROUPS):
                        last = nc.tensor.transpose(ps_w[:, g * P:(g + 1) * P], ctx_t[:, g, i * P:(i + 1) * P], ident[:])
                    last.then_inc(w_full, 1)
                if kind == "cb":
                    pe.wait_ge(w_read, count(w * 8 + 4 + i))
                    for t in range(TILES):
                        last = nc.tensor.transpose(ps_w[:, t * P:(t + 1) * P], ctx_tok[:, t, i * P:(i + 1) * P], ident[:])
                    last.then_inc(w_full, 1)
                if kind == "wo":
                    pe.wait_ge(w_read, count(w * 8 + 6 + i))
                    for h in range(2):
                        t = slice((2 * i + h) * P, (2 * i + h + 1) * P)
                        last = three_products(ps_w[:, h * DIM:(h + 1) * DIM], [
                            (ct_hi[:, c, t], ct_lo[:, c, t], w_hi[:, 3, c], w_lo[:, 3, c]) for c in range(CH)])
                    last.then_inc(w_full, 1)
                if kind == "nm":
                    pe.wait_ge(max_read, count(a * 32 + 32))
                    wait(pe, w_read, (w + 1) * 8)
                    for t in range(TILES):
                        last = nc.tensor.transpose(ps_w[:, t * P:(t + 1) * P], mx[:, t, :], ident[:])
                    last.then_inc(nm_full, 1)

            def slot(s, e, has_a, has_e, has_w, has_prev):
                for u in range(BEFORE, BEHIND + 1):
                    if has_e and 0 <= u < STEPS:
                        scores_for_exp(s, e, u)
                        if u % 4 == 1 and u >= 4:
                            probs_times_values(s, e, u // 4 - 1)
                    if has_a:
                        for n in maxima_of(u):
                            scores_for_max(s + 1, e, n)
                    for kind, i in SIDE.get(u, ()):
                        if kind == "pv":
                            if has_prev:
                                probs_times_values(s - 1, 1 - e, 15)
                        elif has_a if kind in INPUT_SIDE else has_w:
                            side(kind, i, s + 1, s - 1)

            slots(pe, slot)

        @block.scalar
        def _(act):
            act.wait_ge(const_in, 16 * 11)
            act.wait_ge(weight_hi, 5)

            def exponential(b, e, u):
                tick = u // 4
                if u % 4 == 0:
                    wait(act, pv_done, b * 16 + tick - 1)
                act.wait_ge(exp_full, count(b * STEPS + u + 1))
                nc.scalar.activation(probs[:, u % 8, :], ps_exp[u % 2][:], ACT.Exp).then_inc(exp_done, 1)

            def keep_context(b, g):
                act.wait_ge(pv_done, count(b * 16 + 4 * g + 4))
                if g == 0:
                    wait(act, w_full, b * 8 - 4)
                nc.scalar.activation(ctx_t[:, g, :], ps_pv[:], ACT.Copy).then_inc(ctx_kept, 1)

            def middle_part(a, i):
                act.wait_ge(a_read, count(a * 8 + 3 + i))
                nc.scalar.activation(parts[i % 2][:, 1, i // 2, :], rest[:, i], ACT.Copy).then_inc(part_m, 1)

            def side(kind, i, a, w):
                if kind == "xt":
                    act.wait_ge(a_full, count(a * 8 + i + 1))
                    nc.scalar.activation(xt_hi[:, i], ps_a[i], ACT.Copy).then_inc(a_high, 1)
                if kind == "proj":
                    act.wait_ge(a_full, count(a * 8 + 3 + i))
                    k, f = i % 2, i // 2
                    wait(act, saved[k][f], a * 48)
                    nc.scalar.activation(parts[k][:, 0, f, :], ps_a[i % 2], ACT.Identity,
                                         bias=b_qk[:, k, f:f + 1]).then_inc(a_high, 1)
                if kind == "cb":
                    act.wait_ge(w_full, count(w * 8 + 5 + i))
                    nc.scalar.activation(ct_hi[:, i], ps_w[:], ACT.Copy).then_inc(w_part, 1)

            def slot(s, e, has_a, has_e, has_w, has_prev):
                a = s + 1
                for u in range(BEFORE, BEHIND + 1):
                    if has_e and 0 <= u < STEPS:
                        exponential(s, e, u)
                        if u % 16 == 2 and u > 16:
                            keep_context(s, u // 16 - 1)
                    for kind, i in SIDE.get(u, ()):
                        if kind == "pv":
                            if has_prev:
                                keep_context(s - 1, GROUPS - 1)
                        elif (kind in ("xt", "proj") and has_a) or (kind == "cb" and has_w):
                            side(kind, i, s + 1, s - 1)
                            if kind == "proj" and i > 0:
                                middle_part(a, i - 1)
                            if kind == "proj" and i == 3:
                                middle_part(a, i)

            slots(act, slot)

        @block.vector
        def _(dve):
            nc.vector.memset(mx[:], 0.0).then_inc(cleared, 1)
            for i in range(2):
                nc.vector.memset(vals[i][:], 0.0).then_inc(cleared, 1)
            dve.wait_ge(cleared, 3)
            for i in range(2):
                nc.vector.memset(vals[i][:, :, :, HEAD_DIM:HEAD_DIM + 1], 1.0).then_inc(cleared, 1)
            dve.wait_ge(const_in, 16 * 11)
            for i in range(4):
                scale = QSCALE if i == 0 else 1.0
                dve.wait_ge(weight_in, 16 * i + 16)
                nc.vector.tensor_scalar(w_hi[:, i], w_raw[:], scale, None, ALU.mult).then_inc(weight_hi, 1)
                dve.wait_ge(weight_hi, i + 1)
                nc.vector.scalar_tensor_tensor(out=w_lo[:, i], in0=w_raw[:], scalar=scale, in1=w_hi[:, i].bitcast(F32),
                                               op0=ALU.mult, op1=ALU.subtract).then_inc(weight_lo, 1)
            nc.vector.tensor_scalar(b_qk[:, 0], b_qk[:, 0], QSCALE, None, ALU.mult).then_inc(weight_hi, 1)
            dve.wait_ge(weight_hi, 5)

            def row_max(a, n):
                head, half = n // 2, n % 2
                if n == 0:
                    wait(dve, nm_full, a)
                dve.wait_ge(max_full, count(a * 32 + n + 1))
                nc.vector.tensor_reduce(mx[:, 2 * half:2 * half + 2, head:head + 1], ps_max[n % 2][:], AX_X, ALU.max).then_inc(max_read, 1)

            def low_part(a, i):
                dve.wait_ge(part_m, count(a * 4 + i + 1))
                nc.vector.tensor_tensor(parts[i % 2][:, 2, i // 2, :], rest[:, i], parts[i % 2][:, 1, i // 2, :],
                                        ALU.subtract).then_inc(part_l[i % 2], 1)

            def side(kind, i, a, w, e):
                if kind == "xt":
                    dve.wait_ge(a_high, count(a * 6 + i + 1))
                    nc.vector.tensor_tensor(xt_lo[:, i], ps_a[i], xt_hi[:, i].bitcast(F32), ALU.subtract).then_inc(a_read, 1)
                if kind == "proj":
                    k, f = i % 2, i // 2
                    dve.wait_ge(a_high, count(a * 6 + 3 + i))
                    if k == 0:
                        wait(dve, part_l[0], a * CH + f - 1)
                    nc.vector.scalar_tensor_tensor(out=rest[:, i], in0=ps_a[i % 2], scalar=b_qk[:, k, f:f + 1],
                                                   in1=parts[k][:, 0, f, :], op0=ALU.add, op1=ALU.subtract).then_inc(a_read, 1)
                if kind == "v":
                    dve.wait_ge(a_full, count(a * 8 + 7 + i))
                    if i == 0:
                        wait(dve, pv_done, (a - 1) * 16)
                    nc.vector.tensor_tensor(
                        vals[1 - e][:, 2 * i:2 * i + 2, :, 0:HEAD_DIM],
                        ps_a[i].rearrange("p (t h d) -> p t h d", t=2, h=HEADS),
                        bv[:].rearrange("p (a h d) -> p a h d", a=1, h=HEADS).to_broadcast([P, 2, HEADS, HEAD_DIM]),
                        ALU.add).then_inc(a_read, 1)
                if kind == "ct":
                    dve.wait_ge(w_full, count(w * 8 + i + 1))
                    rows = ps_w[:].rearrange("p (h d) -> p h d", d=32)
                    nc.vector.reciprocal(inv[:, i, :].rearrange("p (h a) -> p h a", a=1), rows[:, :, HEAD_DIM:HEAD_DIM + 1]).then_inc(w_part, 1)
                    dve.wait_ge(w_part, count(w * 6 + i + 1))
                    nc.vector.tensor_tensor(
                        ctx_tok[:, i, :].rearrange("p (h d) -> p h d", d=HEAD_DIM), rows[:, :, 0:HEAD_DIM],
                        inv[:, i, :].rearrange("p (h a) -> p h a", a=1).to_broadcast([P, HEADS, HEAD_DIM]),
                        ALU.mult).then_inc(w_read, 1)
                if kind == "cb":
                    dve.wait_ge(w_part, count(w * 6 + 5 + i))
                    nc.vector.tensor_tensor(ct_lo[:, i], ps_w[:], ct_hi[:, i].bitcast(F32), ALU.subtract).then_inc(w_read, 1)
                if kind == "wo":
                    dve.wait_ge(w_full, count(w * 8 + 7 + i))
                    if i == 0:
                        dve.wait_ge(xres_ready, count(w + 1))
                        wait(dve, ln_done, w)
                    nc.vector.tensor_tensor(res[:, 2 * i:2 * i + 2, :], ps_w[:].rearrange("p (t d) -> p t d", t=2),
                                            x_res[:, 2 * i:2 * i + 2, :], ALU.add).then_inc(w_read, 1)
                if kind == "ln":
                    dve.wait_ge(w_read, count(w * 8 + 8))
                    for t in range(TILES):
                        nc.vector.bn_stats(stats[:, t, :], res[:, t, :]).then_inc(ln_stats, 1)
                    for t in range(TILES):
                        dve.wait_ge(ln_stats, count(w * TILES + t + 1))
                        dve.sem_inc(dve_through)
                        nc.vector.bn_aggr(moments[:, t, :], stats[:, t, :]).then_inc(ln_moments, 1)
                if kind == "norm":
                    dve.wait_ge(ln_rstd, count(w * 2 + 2))
                    wait(dve, y_saved, w * 16)
                    for t in range(TILES):
                        last = nc.vector.tensor_scalar(normed[:, t, :], res[:, t, :], moments[:, t, 0:1], rstd[:, t:t + 1],
                                                       ALU.subtract, ALU.mult)
                    last.then_inc(ln_done, 1)
                if kind == "nm":
                    dve.wait_ge(nm_full, count(a + 1))
                    wait(dve, m_saved, a * 16)
                    nc.vector.tensor_scalar(m_parts[:, 0, :], ps_w[0:HEADS, :], -1.0, None, ALU.mult).then_inc(nm_high, 1)
                    dve.wait_ge(nm_high, count(a + 1))
                    nc.vector.scalar_tensor_tensor(out=m_parts[:, 1, :], in0=ps_w[0:HEADS, :], scalar=-1.0, in1=m_parts[:, 0, :],
                                                   op0=ALU.mult, op1=ALU.subtract).then_inc(nm_read, 1)

            def slot(s, e, has_a, has_e, has_w, has_prev):
                a = s + 1
                for u in range(BEFORE, BEHIND + 1):
                    if has_a:
                        for n in maxima_of(u):
                            row_max(a, n)
                    for kind, i in SIDE.get(u, ()):
                        if kind != "pv" and (has_a if kind in INPUT_SIDE else has_w):
                            side(kind, i, a, s - 1, e)
                            if kind == "proj" and i == 2:
                                low_part(a, 1)
                            if kind == "proj" and i == 3:
                                low_part(a, 3)

            slots(dve, slot)

        @block.gpsimd
        def _(pool):
            nc.gpsimd.memset(power[:], -0.5).then_inc(power_set, 1)
            pool.wait_ge(const_in, 16 * 11)
            pool.wait_ge(power_set, 1)

            def slot(s, e, has_a, has_e, has_w, has_prev):
                a, w = s + 1, s - 1
                if has_w:
                    pool.wait_ge(xres_in, count(w * 16 + 16))
                    nc.gpsimd.tensor_tensor(x_res[:], x_res[:], bo[:].rearrange("p (a d) -> p a d", a=1).to_broadcast([P, TILES, DIM]),
                                            ALU.add).then_inc(xres_ready, 1)
                if has_a:
                    for f in range(CH):
                        pool.wait_ge(part_m, count(a * 4 + 2 * f + 1))
                        nc.gpsimd.tensor_tensor(parts[0][:, 2, f, :], rest[:, 2 * f], parts[0][:, 1, f, :],
                                                ALU.subtract).then_inc(part_l[0], 1)
                if has_w:
                    pool.wait_ge(ln_moments, count(w * TILES + TILES))
                    pool.sem_inc(pool_through)
                    nc.gpsimd.tensor_scalar(rstd[:].rearrange("p (t a) -> p t a", a=1), moments[:, :, 1:2], EPS, None, ALU.add).then_inc(ln_rstd, 1)
                    pool.wait_ge(ln_rstd, count(w * 2 + 1))
                    nc.gpsimd.tensor_tensor(rstd[:], rstd[:], power[:], ALU.pow).then_inc(ln_rstd, 1)

            slots(pool, slot)


SECOND_BEHIND = ((2,), (), (3,), (4,), (), (5,), (), (6, 7))


EPILOGUE_BEHIND = (3, 5, 7)


def feed_forward(nc, io, y1, out):
    with ExitStack() as ctx:
        def sb(name, shape, dt=F32):
            return ctx.enter_context(nc.sbuf_tensor(name, shape, dt))

        def ps(name, shape):
            return ctx.enter_context(nc.psum_tensor(name, shape, F32))

        def sem(name):
            return ctx.enter_context(nc.semaphore(name))

        ident = sb("f_ident", [P, P])
        w1_raw = sb("w1_raw", [P, CH, HIDDEN])
        w2_raw = sb("w2_raw", [P, HC, DIM])
        w1_hi = sb("w1_hi", [P, CH, HIDDEN], F32R)
        w1_lo = sb("w1_lo", [P, CH, HIDDEN], F32R)
        w2_hi = sb("w2_hi", [P, HC, DIM], F32R)
        w2_lo = sb("w2_lo", [P, HC, DIM], F32R)
        wr_raw = sb("wr_raw", [EXPERTS, DIM])
        wr_hi = sb("wr_hi", [P, CH, EXPERTS], F32R)
        wr_lo = sb("wr_lo", [P, CH, EXPERTS], F32R)
        b1_raw = sb("b1_raw", [HC, P])
        b1 = sb("b1", [P, HC])
        b2 = sb("b2", [P, DIM])
        y_turn = [sb(f"rows_to_turn{i}", [P, TILES, DIM]) for i in range(2)]
        y_res = [sb(f"residual_rows{i}", [P, TILES, DIM]) for i in range(2)]
        yt_hi = sb("yt_hi", [P, CH, SEQ], F32R)
        yt_lo = sb("yt_lo", [P, CH, SEQ], F32R)
        act_out = sb("act_out", [P, 4, SEQ])
        h_hi = [sb(f"h_hi{i}", [P, HC, SEQ], F32R) for i in range(2)]
        h_lo = [sb(f"h_lo{i}", [P, HC, SEQ], F32R) for i in range(2)]
        top = sb("top", [P, TILES])
        shifted = sb("shifted", [P, TILES, EXPERTS])
        expd = sb("expd", [P, TILES, EXPERTS])
        total = sb("total", [P, TILES])
        inv = sb("f_inv", [P, TILES])
        gate = [sb(f"gate{i}", [P, TILES]) for i in range(2)]
        ffn = sb("ffn", [P, TILES, DIM])
        res = sb("f_res", [P, TILES, DIM])
        stats = sb("f_stats", [P, TILES, 6])
        moments = sb("f_moments", [P, TILES, 2])
        rstd = sb("f_rstd", [P, TILES])
        power = sb("f_power", [P, TILES])
        normed = sb("f_normed", [P, TILES, DIM])

        ps_t = [ps(f"ps_t{i}", [P, SEQ]) for i in range(2)]
        ps_r = ps("ps_r", [P, TILES, EXPERTS])
        ps_1 = [ps(f"ps_1{i}", [P, SEQ]) for i in range(2)]
        ps_2 = [ps(f"ps_2{i}", [P, 2, DIM]) for i in range(2)]

        const_in = sem("f_const_in")
        b2_in = sem("b2_in")
        w1_in = sem("w1_in")
        w2_in = sem("w2_in")
        wr_high = sem("wr_high")
        wr_low = sem("wr_low")
        w1_high = sem("w1_high")
        w1_low = sem("w1_low")
        w2_high = sem("w2_high")
        w2_low = sem("w2_low")
        wr_turned = sem("wr_turned")
        b1_ready = sem("b1_ready")
        y_turn_in = [sem(f"y_turn_in{i}") for i in range(2)]
        y_res_in = [sem(f"y_res_in{i}") for i in range(2)]
        t_full = sem("t_full")
        t_high = sem("t_high")
        t_read = sem("t_read")
        r_full = sem("r_full")
        r_step = sem("r_step")
        r_exp = sem("r_exp")
        f1_full = sem("f1_full")
        f1_act = sem("f1_act")
        h_high = sem("h_high")
        h_low = [sem(f"h_low{i}") for i in range(2)]
        f2_full = sem("f2_full")
        f2_read = sem("f2_read")
        gated = sem("gated")
        ln_stats = sem("f_ln_stats")
        ln_moments = sem("f_ln_moments")
        pool_through = sem("f_pool_through")
        dve_through = sem("f_dve_through")
        power_set = sem("f_power_set")
        ln_rstd = sem("f_ln_rstd")
        ln_done = sem("f_ln_done")
        out_saved = sem("out_saved")

        y_view = y1.rearrange("b (t p) d -> b p t d", p=P)
        out_view = out.rearrange("b (t p) d -> b p t d", p=P)
        last_expert = EXPERTS - 1
        w1_view = io["L0_ffn_W1"][last_expert].rearrange("(c p) f -> p c f", p=P)
        w2_view = io["L0_ffn_W2"][last_expert].rearrange("(c p) n -> p c n", p=P)

        block = ctx.enter_context(nc.Block())

        def slots(eng, slot):
            slot(-1, 1, True, False)
            slot(0, 0, True, True)
            with eng.Fori(0, (BATCH - 2) // 2) as pair:
                slot(Linear(pair, 2, 1), 1, True, True)
                slot(Linear(pair, 2, 2), 0, True, True)
            slot(BATCH - 1, 1, False, True)


        @block.sync
        def _(sync):
            sync.dma_start(ident[:], io["identity"]).then_inc(const_in, 16)
            sync.dma_start(wr_raw[:], io["L0_ffn_Wr"]).then_inc(const_in, 16)
            sync.dma_start(b1_raw[:], io["L0_ffn_b1"][last_expert].rearrange("(c p) -> c p", p=P)).then_inc(const_in, 16)
            sync.dma_start(y_turn[0][:], y_view[0]).then_inc(y_turn_in[0], 16)
            sync.dma_start(w1_raw[:], w1_view).then_inc(w1_in, 16)
            sync.dma_start(y_turn[1][:], y_view[1]).then_inc(y_turn_in[1], 16)
            sync.dma_start(w2_raw[:], w2_view).then_inc(w2_in, 16)
            sync.dma_start(b2[:], io["L0_ffn_b2"][last_expert].partition_broadcast(P)).then_inc(b2_in, 16)

            def slot(s, e, has_n, has_f):
                if has_n:
                    if has_f:
                        wait(sync, gated, s * TILES)
                    sync.dma_start(y_res[1 - e][:], y_view[count(s + 1)]).then_inc(y_res_in[1 - e], 16)
                    sync.wait_ge(t_full, count(s * CH + 2 * CH))
                    sync.dma_start(y_turn[1 - e][:], y_view[count(s + 3) % BATCH]).then_inc(y_turn_in[1 - e], 16)
                if has_f and not (isinstance(s, int) and s == 0):
                    store(s - 1)

            def store(w):
                sync.wait_ge(ln_done, count(w + 1))
                sync.dma_start(out_view[count(w)], normed[:]).then_inc(out_saved, 16)

            slots(sync, slot)
            store(BATCH - 1)
            sync.wait_ge(out_saved, BATCH * 16)

        @block.tensor
        def _(pe):
            pe.wait_ge(const_in, 16 * 3)
            for c in range(CH):
                last = nc.tensor.transpose(ps_r[:].rearrange("p t x -> p (t x)")[:, c * EXPERTS:(c + 1) * EXPERTS],
                                           wr_raw[:, c * P:(c + 1) * P], ident[0:EXPERTS, 0:EXPERTS])
            last.then_inc(wr_turned, 1)
            nc.tensor.transpose(ps_t[0][:, 0:HC], b1_raw[:], ident[0:HC, 0:HC]).then_inc(wr_turned, 1)
            pe.wait_ge(b1_ready, 1)

            def turn_rows(n, e, c):
                if c == 0:
                    pe.wait_ge(y_turn_in[1 - e], count(n * 8 + (16 - 8 * (1 - e))))
                wait(pe, t_read, n * 2 + c - 1)
                for t in range(TILES):
                    last = nc.tensor.transpose(ps_t[c][:, t * P:(t + 1) * P], y_turn[1 - e][:, t, c * P:(c + 1) * P], ident[:])
                last.then_inc(t_full, 1)

            def router(n):
                pe.wait_ge(t_read, count(n * 2 + 2))
                wait(pe, r_step, n * 5 - 3)
                pe.wait_ge(wr_low, 1)
                for t in range(TILES):
                    i = 0
                    for c in range(CH):
                        ts = slice(t * P, (t + 1) * P)
                        for l, r in ((yt_hi, wr_hi), (yt_hi, wr_lo), (yt_lo, wr_hi)):
                            last = nc.tensor.matmul(ps_r[:, t, :], l[:, c, ts], r[:, c, :], start=i == 0, stop=i == 5)
                            i += 1
                last.then_inc(r_full, 1)

            def first_product(n, i):
                wait(pe, f1_act, n * HC + i - 1)
                if i == 0:
                    pe.wait_ge(w1_low, 1)
                k = 0
                for c in range(CH):
                    for l, r in ((w1_hi, yt_hi), (w1_hi, yt_lo), (w1_lo, yt_hi)):
                        last = nc.tensor.matmul(ps_1[i % 2][:], l[:, c, i * P:(i + 1) * P], r[:, c, :], start=k == 0, stop=k == 5)
                        k += 1
                last.then_inc(f1_full, 1)

            def second_product(s, e, i):
                t = i // 2
                ts = slice(t * P, (t + 1) * P)
                if i == 0:
                    pe.wait_ge(h_low[0], count(s * 4 + 4))
                    pe.wait_ge(h_low[1], count(s * 4 + 4))
                    pe.wait_ge(w2_low, 1)
                if i % 2 == 0:
                    wait(pe, f2_read, s * TILES + t - 1)
                for c in range(4 * (i % 2), 4 * (i % 2) + 4):
                    for l, r in ((h_hi, w2_hi), (h_hi, w2_lo), (h_lo, w2_hi)):
                        last = nc.tensor.matmul(ps_2[t % 2][:, t // 2, :], l[e][:, c, ts], r[:, c, :],
                                                start=c == 0 and l is h_hi and r is w2_hi, stop=c == HC - 1 and l is h_lo)
                if i % 2:
                    last.then_inc(f2_full, 1)

            def slot(s, e, has_n, has_f):
                if has_n:
                    turn_rows(s + 1, e, 0)
                    turn_rows(s + 1, e, 1)
                if has_f:
                    second_product(s, e, 0)
                    second_product(s, e, 1)
                if has_n:
                    router(s + 1)
                for i in range(HC):
                    if has_n:
                        first_product(s + 1, i)
                    if has_f:
                        for half in SECOND_BEHIND[i]:
                            second_product(s, e, half)

            slots(pe, slot)

        @block.scalar
        def _(act):
            act.wait_ge(w1_in, 16)
            nc.scalar.activation(w1_hi[:], w1_raw[:], ACT.Copy).then_inc(w1_high, 1)
            act.wait_ge(b1_ready, 1)

            def slot(s, e, has_n, has_f):
                n = s + 1
                if not has_n:
                    return
                for c in range(CH):
                    act.wait_ge(t_full, count(n * 2 + c + 1))
                    nc.scalar.activation(yt_hi[:, c], ps_t[c][:], ACT.Copy).then_inc(t_high, 1)
                act.wait_ge(r_step, count(n * 5 + 2))
                nc.scalar.activation(expd[:], shifted[:], ACT.Exp).then_inc(r_exp, 1)
                for i in range(HC):
                    act.wait_ge(f1_full, count(n * HC + i + 1))
                    wait(act, h_low[i % 2], n * 4 + i // 2 - 1)
                    nc.scalar.activation(act_out[:, i % 4, :], ps_1[i % 2][:], ACT.Gelu, bias=b1[:, i:i + 1]).then_inc(f1_act, 1)

            slots(act, slot)

        @block.vector
        def _(dve):
            dve.wait_ge(wr_turned, 1)
            turned = ps_r[:].rearrange("p t x -> p (t x)")[:, 0:CH * EXPERTS].rearrange("p (c x) -> p c x", c=CH)
            nc.vector.tensor_copy(wr_hi[:], turned).then_inc(wr_high, 1)
            dve.wait_ge(wr_turned, 2)
            nc.vector.tensor_copy(b1[:], ps_t[0][:, 0:HC]).then_inc(b1_ready, 1)
            dve.wait_ge(wr_high, 1)
            nc.vector.tensor_tensor(wr_lo[:], turned, wr_hi[:].bitcast(F32), ALU.subtract).then_inc(wr_low, 1)
            dve.wait_ge(w1_high, 1)
            nc.vector.tensor_tensor(w1_lo[:], w1_raw[:], w1_hi[:].bitcast(F32), ALU.subtract).then_inc(w1_low, 1)

            def column(x):
                return x.rearrange("p (t a) -> p t a", a=1)

            def epilogue(s, e, t):
                dve.wait_ge(f2_full, count(s * TILES + t + 1))
                if isinstance(s, int) and s == 0 and t == 0:
                    dve.wait_ge(b2_in, 16)
                nc.vector.tensor_tensor(ffn[:, t, :], ps_2[t % 2][:, t // 2, :], b2[:], ALU.add).then_inc(f2_read, 1)
                dve.wait_ge(f2_read, count(s * TILES + t + 1))
                wait(dve, ln_done, s)
                if t == 0:
                    dve.wait_ge(y_res_in[e], count(s * 8 + (16 - 8 * e)))
                nc.vector.scalar_tensor_tensor(out=res[:, t, :], in0=ffn[:, t, :], scalar=gate[e][:, t:t + 1], in1=y_res[e][:, t, :],
                                               op0=ALU.mult, op1=ALU.add).then_inc(gated, 1)
                dve.wait_ge(gated, count(s * TILES + t + 1))
                nc.vector.bn_stats(stats[:, t, :], res[:, t, :]).then_inc(ln_stats, 1)
                dve.wait_ge(ln_stats, count(s * TILES + t + 1))
                dve.sem_inc(dve_through)
                nc.vector.bn_aggr(moments[:, t, :], stats[:, t, :]).then_inc(ln_moments, 1)

            def normalise(w):
                if isinstance(w, int) and w < 0:
                    return
                wait(dve, out_saved, w * 16)
                for t in range(TILES):
                    last = nc.vector.tensor_scalar(normed[:, t, :], res[:, t, :], moments[:, t, 0:1], rstd[:, t:t + 1],
                                                   ALU.subtract, ALU.mult)
                last.then_inc(ln_done, 1)

            def slot(s, e, has_n, has_f):
                n = s + 1
                if has_n:
                    for c in range(CH):
                        dve.wait_ge(t_high, count(n * 2 + c + 1))
                        nc.vector.tensor_tensor(yt_lo[:, c], ps_t[c][:], yt_hi[:, c].bitcast(F32), ALU.subtract).then_inc(t_read, 1)
                if not has_f:
                    dve.wait_ge(w2_in, 16)
                    nc.vector.tensor_copy(w2_hi[:], w2_raw[:]).then_inc(w2_high, 1)
                if has_f:
                    wait(dve, ln_rstd, s * 2)
                    normalise(s - 1)
                    epilogue(s, e, 0)
                if has_n:
                    dve.wait_ge(r_full, count(n + 1))
                    nc.vector.tensor_reduce(top[:], ps_r[:], AX_X, ALU.max).then_inc(r_step, 1)
                    dve.wait_ge(r_step, count(n * 5 + 1))
                    nc.vector.tensor_tensor(shifted[:], ps_r[:], column(top[:]).to_broadcast([P, TILES, EXPERTS]),
                                            ALU.subtract).then_inc(r_step, 1)
                for i in range(HC):
                    if has_n:
                        dve.wait_ge(f1_act, count(n * HC + i + 1))
                        nc.vector.tensor_copy(h_hi[1 - e][:, i, :], act_out[:, i % 4, :]).then_inc(h_high, 1)
                        if i % 2:
                            dve.wait_ge(h_high, count(n * HC + i + 1))
                            nc.vector.tensor_tensor(h_lo[1 - e][:, i, :], act_out[:, i % 4, :], h_hi[1 - e][:, i, :].bitcast(F32),
                                                    ALU.subtract).then_inc(h_low[1], 1)
                    if has_n and i == 0:
                        dve.wait_ge(r_exp, count(n + 1))
                        nc.vector.tensor_reduce(total[:], expd[:], AX_X, ALU.add).then_inc(r_step, 1)
                        dve.wait_ge(r_step, count(n * 5 + 3))
                        nc.vector.reciprocal(inv[:], total[:]).then_inc(r_step, 1)
                        dve.wait_ge(r_step, count(n * 5 + 4))
                        nc.vector.tensor_tensor(column(gate[1 - e][:]), expd[:, :, last_expert:EXPERTS], column(inv[:]),
                                                ALU.mult).then_inc(r_step, 1)
                    if has_f and i in EPILOGUE_BEHIND:
                        epilogue(s, e, EPILOGUE_BEHIND.index(i) + 1)

            slots(dve, slot)
            dve.wait_ge(ln_rstd, BATCH * 2)
            normalise(BATCH - 1)

        @block.gpsimd
        def _(pool):
            nc.gpsimd.memset(power[:], -0.5).then_inc(power_set, 1)
            pool.wait_ge(power_set, 1)
            pool.wait_ge(w2_high, 1)
            nc.gpsimd.tensor_tensor(w2_lo[:], w2_raw[:], w2_hi[:].bitcast(F32), ALU.subtract).then_inc(w2_low, 1)

            def slot(s, e, has_n, has_f):
                n = s + 1
                if has_n:
                    for i in range(0, HC, 2):
                        pool.wait_ge(h_high, count(n * HC + i + 1))
                        nc.gpsimd.tensor_tensor(h_lo[1 - e][:, i, :], act_out[:, i % 4, :], h_hi[1 - e][:, i, :].bitcast(F32),
                                                ALU.subtract).then_inc(h_low[0], 1)
                if has_f:
                    pool.wait_ge(ln_moments, count(s * TILES + TILES))
                    pool.sem_inc(pool_through)
                    nc.gpsimd.tensor_scalar(rstd[:].rearrange("p (t a) -> p t a", a=1), moments[:, :, 1:2], EPS, None, ALU.add).then_inc(ln_rstd, 1)
                    pool.wait_ge(ln_rstd, count(s * 2 + 1))
                    nc.gpsimd.tensor_tensor(rstd[:], rstd[:], power[:], ALU.pow).then_inc(ln_rstd, 1)

            slots(pool, slot)


def build(nc, io, out):
    y1 = nc.dram_tensor("attn_out", [BATCH, SEQ, DIM], F32, kind="Internal").ap()
    q_parts = nc.dram_tensor("q_parts_dram", [HEADS, 3, HEAD_DIM, SEQ], BF16, kind="Internal").ap()
    k_parts = nc.dram_tensor("k_parts_dram", [HEADS, 3, HEAD_DIM, SEQ], BF16, kind="Internal").ap()
    m_parts = nc.dram_tensor("m_parts_dram", [HEADS, 2, SEQ], BF16, kind="Internal").ap()
    attention(nc, io, y1, q_parts, k_parts, m_parts)
    feed_forward(nc, io, y1, out)


_INS = ['L0_attn_inputs', 'L0_attn_Wq', 'L0_attn_bq', 'L0_attn_Wk', 'L0_attn_bk', 'L0_attn_Wv', 'L0_attn_bv',
        'L0_attn_Wo', 'L0_attn_bo', 'L0_ffn_Wr', 'L0_ffn_W1', 'L0_ffn_b1', 'L0_ffn_W2', 'L0_ffn_b2']


def constants():
    import numpy as np

    base = (2.0 ** 8) ** (1.0 / HEADS)
    slopes = np.asarray([1.0 / base ** (i + 1) for i in range(HEADS)], np.float32)
    bias = slopes[:, None] * np.arange(SEQ, dtype=np.float32)[None, :]
    rows = np.full((6, HEADS, SEQ), 0x3F80, np.uint16)
    for r in range(3):
        upper = bias.view(np.uint32) & np.uint32(0xFFFF0000)
        rows[r] = upper >> 16
        bias = bias - upper.view(np.float32)
    return {"identity": np.eye(P, dtype=np.float32), "rows": rows}


def kernel(**inputs):
    import numpy as np
    import concourse.bacc as bacc
    from concourse.bass_utils import run_bass_kernel_spmd

    nc = bacc.Bacc("TRN2", target_bir_lowering=False, num_devices=1)
    nc.disable_value_cache = True
    arrays, io = {}, {}
    for name, a in [(n, inputs[n]) for n in _INS] + list(constants().items()):
        a = np.ascontiguousarray(a)
        arrays[f"in_{name}"] = a
        io[name] = nc.dram_tensor(f"in_{name}", a.shape, mybir.dt.from_np(a.dtype), kind="ExternalInput").ap()
    out = nc.dram_tensor("out", (BATCH, SEQ, DIM), F32, kind="ExternalOutput").ap()
    build(nc, io, out)
    r = run_bass_kernel_spmd(nc, [arrays], core_ids=[0])
    return r.results[0]["out"]
```
